# Optimizing a Trainium2 kernel written in Bass

```python
import numpy as np
import jax
import jax.numpy as jnp

def _softmax(x, axis=-1):
    return jax.nn.softmax(x, axis=axis)

def _gelu(x):
    return jax.nn.gelu(x, approximate=True)

def _silu(x):
    return jax.nn.silu(x)

def _sigmoid(x):
    return jax.nn.sigmoid(x)

def _layernorm(x, axis=-1, eps=1e-05):
    m = jnp.mean(x, axis=axis, keepdims=True)
    v = jnp.var(x, axis=axis, keepdims=True)
    return (x - m) / jnp.sqrt(v + eps)

def _scatter_add(tgt, idx, src, axis=0):
    return tgt.at[idx].add(src)

def _segment_sum(src, seg, n):
    return jax.ops.segment_sum(src, seg, n)
kernel_name = 'mk_gnn_resnorm_d2_gnn_r8_7ce8ce'

def setup_inputs(seed: int=0):
    np.random.seed(seed)
    _w = jnp.asarray

    def _rec_inputs():
        import jax
        import jax.numpy as jnp
        _gk = jax.random.key(seed)
        x = -0.0003713 + 1 * jax.random.normal(jax.random.fold_in(_gk, 1), (6250, 128), jnp.float32)
        _s = jax.random.randint(jax.random.fold_in(_gk, 2), (100000,), 0, 6250, jnp.int32)
        _d = jax.random.randint(jax.random.fold_in(_gk, 3), (100000,), 0, 6250, jnp.int32)
        _loop = jnp.arange(6250, dtype=jnp.int32)
        src = jnp.concatenate([_s, _d, _loop])
        dst = jnp.concatenate([_d, _s, _loop])
        _o = jnp.argsort(dst, stable=True)
        src = src[_o]
        dst = dst[_o]
        edge_attr_16 = 0.000196303 + 1.00016 * jax.random.normal(jax.random.fold_in(_gk, 11), (206250, 16), jnp.float32)
        edge_attr_32 = jax.random.uniform(jax.random.fold_in(_gk, 12), (206250, 32), jnp.float32, 0.0, 1)
        edge_weight = jax.random.uniform(jax.random.fold_in(_gk, 14), (206250,), jnp.float32, 0.0, 0.999999)
        return (x, src, dst, edge_attr_16, edge_attr_32, edge_weight)
    x, src, dst, edge_attr_16, edge_attr_32, edge_weight = _rec_inputs()

    def _L0_gnn_setup():
        import jax, jax.numpy as jnp
        import numpy as np
        LOG2 = float(np.log(2.0))

        def ssp(v):
            return jax.nn.softplus(v) - jnp.asarray(LOG2, v.dtype)
        key = jax.random.key(seed)
        ks = jax.random.split(key, 16)
        N, B, F, R, P = (12500, 128, 64, 32, 200000)
        inp = {'x': jax.random.normal(ks[0], (N, B), jnp.float32), 'f_ij': jax.random.uniform(ks[1], (P, R), jnp.float32), 'rcut_ij': jax.random.uniform(ks[2], (P,), jnp.float32), 'pairlist': jax.random.randint(ks[3], (2, P), 0, N, jnp.int64), 'w_in': jax.random.normal(ks[4], (B, F), jnp.float32) * (1.0 / np.sqrt(B)), 'b_in': jnp.zeros((F,), jnp.float32), 'w_f1': jax.random.normal(ks[5], (R, F), jnp.float32) * (1.0 / np.sqrt(R)), 'b_f1': jnp.zeros((F,), jnp.float32), 'w_f2': jax.random.normal(ks[6], (F, F), jnp.float32) * (1.0 / np.sqrt(F)), 'b_f2': jnp.zeros((F,), jnp.float32), 'w_o1': jax.random.normal(ks[7], (F, B), jnp.float32) * (1.0 / np.sqrt(F)), 'b_o1': jnp.zeros((B,), jnp.float32), 'w_o2': jax.random.normal(ks[8], (B, B), jnp.float32) * (1.0 / np.sqrt(B)), 'b_o2': jnp.zeros((B,), jnp.float32)}
        return inp
    _L0_gnn_all = _L0_gnn_setup()
    _L0_gnn_in = {k: v for k, v in _L0_gnn_all.items() if k in ('w_in', 'b_in', 'w_f1', 'b_f1', 'w_f2', 'b_f2', 'w_o1', 'b_o1', 'w_o2', 'b_o2')}
    del _L0_gnn_all

    def _L1_gnn_setup():
        import jax, jax.numpy as jnp
        import numpy as np
        N_NODES = 6250
        N_EDGES = 200000
        HIDDEN = 128
        BOND = 16
        key = jax.random.key(seed)
        ks = jax.random.split(key, 6)
        h = jax.random.normal(ks[0], (N_NODES, HIDDEN), dtype=jnp.float32)
        edge_index = jax.random.randint(ks[1], (2, N_EDGES), 0, N_NODES, dtype=jnp.int32)
        bond_features = jax.random.normal(ks[2], (N_EDGES, BOND), dtype=jnp.float32)
        fan_in1 = 2 * HIDDEN + BOND
        W1 = jax.random.normal(ks[3], (fan_in1, HIDDEN), dtype=jnp.float32) / np.sqrt(fan_in1)
        b1 = jnp.zeros((HIDDEN,), dtype=jnp.float32)
        W2 = jax.random.normal(ks[4], (HIDDEN, HIDDEN), dtype=jnp.float32) / np.sqrt(HIDDEN)
        b2 = jnp.zeros((HIDDEN,), dtype=jnp.float32)
        return {'h': h, 'edge_index': edge_index, 'bond_features': bond_features, 'W1': W1, 'b1': b1, 'W2': W2, 'b2': b2}
    _L1_gnn_all = _L1_gnn_setup()
    _L1_gnn_in = {k: v for k, v in _L1_gnn_all.items() if k in ('W1', 'b1', 'W2', 'b2')}
    del _L1_gnn_all
    return {'x': x, 'src': src, 'dst': dst, 'edge_attr_16': edge_attr_16, 'edge_attr_32': edge_attr_32, 'edge_weight': edge_weight, 'L0_gnn_w_in': _L0_gnn_in['w_in'], 'L0_gnn_b_in': _L0_gnn_in['b_in'], 'L0_gnn_w_f1': _L0_gnn_in['w_f1'], 'L0_gnn_b_f1': _L0_gnn_in['b_f1'], 'L0_gnn_w_f2': _L0_gnn_in['w_f2'], 'L0_gnn_b_f2': _L0_gnn_in['b_f2'], 'L0_gnn_w_o1': _L0_gnn_in['w_o1'], 'L0_gnn_b_o1': _L0_gnn_in['b_o1'], 'L0_gnn_w_o2': _L0_gnn_in['w_o2'], 'L0_gnn_b_o2': _L0_gnn_in['b_o2'], 'L1_gnn_W1': _L1_gnn_in['W1'], 'L1_gnn_b1': _L1_gnn_in['b1'], 'L1_gnn_W2': _L1_gnn_in['W2'], 'L1_gnn_b2': _L1_gnn_in['b2']}

def reference(x, src, dst, edge_attr_16, edge_attr_32, edge_weight, L0_gnn_w_in, L0_gnn_b_in, L0_gnn_w_f1, L0_gnn_b_f1, L0_gnn_w_f2, L0_gnn_b_f2, L0_gnn_w_o1, L0_gnn_b_o1, L0_gnn_w_o2, L0_gnn_b_o2, L1_gnn_W1, L1_gnn_b1, L1_gnn_W2, L1_gnn_b2):
    import jax
    import jax.numpy as jnp

    def _L0_gnn_ref(x, f_ij, rcut_ij, pairlist, w_in, b_in, w_f1, b_f1, w_f2, b_f2, w_o1, b_o1, w_o2, b_o2):
        import jax, jax.numpy as jnp
        import numpy as np
        LOG2 = float(np.log(2.0))

        def ssp(v):
            return jax.nn.softplus(v) - jnp.asarray(LOG2, v.dtype)
        n_atoms = x.shape[0]
        h = x @ w_in + b_in
        Wij = ssp(f_ij @ w_f1 + b_f1) @ w_f2 + b_f2
        Wij = Wij * rcut_ij[:, None]
        idx_i, idx_j = (pairlist[0], pairlist[1])
        x_ij = h[idx_j] * Wij
        agg = jax.ops.segment_sum(x_ij, idx_i, num_segments=n_atoms)
        out = ssp(agg @ w_o1 + b_o1) @ w_o2 + b_o2
        return out

    def _L1_gnn_ref(h, edge_index, bond_features, W1, b1, W2, b2):
        import jax, jax.numpy as jnp
        import numpy as np
        N_NODES = 6250
        N_EDGES = 200000
        HIDDEN = 128
        BOND = 16
        row, col = (edge_index[0], edge_index[1])
        msgs = jnp.concatenate([h[row], h[col], bond_features], axis=-1)
        msgs = jax.nn.silu(msgs @ W1 + b1) @ W2 + b2
        h_out = jax.ops.segment_sum(msgs, row, num_segments=h.shape[0])
        return h_out
    edge_index = jnp.stack([src, dst])
    x = _layernorm(x + _L0_gnn_ref(x, edge_attr_32, edge_weight, edge_index, L0_gnn_w_in, L0_gnn_b_in, L0_gnn_w_f1, L0_gnn_b_f1, L0_gnn_w_f2, L0_gnn_b_f2, L0_gnn_w_o1, L0_gnn_b_o1, L0_gnn_w_o2, L0_gnn_b_o2), axis=-1)
    x = _layernorm(x + _L1_gnn_ref(x, edge_index, edge_attr_16, L1_gnn_W1, L1_gnn_b1, L1_gnn_W2, L1_gnn_b2), axis=-1)
    return x

_drawn_inputs = setup_inputs


def setup_inputs(seed=0):
    import zlib

    import numpy as np

    out = dict(_drawn_inputs(seed))
    spreads = {'L0_gnn_b_in': (0.0, 0.1),
     'L0_gnn_b_f1': (0.0, 0.1),
     'L0_gnn_b_f2': (0.0, 0.1),
     'L0_gnn_b_o1': (0.0, 0.1),
     'L0_gnn_b_o2': (0.0, 0.1),
     'L1_gnn_b1': (0.0, 0.1),
     'L1_gnn_b2': (0.0, 0.1)}
    factors = {}
    for name, (base, spread) in spreads.items():
        noise = np.random.default_rng([zlib.crc32(name.encode()), seed]).standard_normal(out[name].shape)
        drawn = base * np.exp(spread * noise) if base else spread * noise
        out[name] = jnp.asarray(drawn.astype(out[name].dtype))
    for name, factor in factors.items():
        out[name] = (out[name] * factor).astype(out[name].dtype)
    return out
```

```python
from contextlib import ExitStack

import numpy as np

import concourse.bass as bass
from concourse import mybir

ALU = mybir.AluOpType
ACT = mybir.ActivationFunctionType
F32 = mybir.dt.float32
I32 = mybir.dt.int32
BF16 = mybir.dt.bfloat16
X = mybir.AxisListType.X
PE_ONLY = (mybir.EngineType.PE,)
DVE_ONLY = (mybir.EngineType.DVE,)

P = 128
NODES, HID, FILT, RBF, BOND = 6250, 128, 64, 32, 16
EDGES = 206250
NB = HID - BOND
BLOCKS = -(-NODES // NB)
STEP = 8
SE = STEP * P
TILES = -(-EDGES // (2 * SE)) * 2 * STEP
STEPS = TILES // STEP
PADDED = TILES * P
SLOT_TILES = -(-(TILES + BLOCKS) // (2 * STEP)) * 2 * STEP
SLOT_STEPS = SLOT_TILES // STEP
SLOTS = SLOT_TILES * P
TC = -(-SLOT_TILES // P)
REC = FILT + 1 + BOND + 2
R_ONE, R_BOND, R_META = FILT, FILT + 1, FILT + 1 + BOND
MSG = FILT + 1
NPAD = BLOCKS * NB
NT = NPAD // P
assert NPAD == NT * P and TILES * P == PADDED
PER_BANK = 512 // MSG
BANKS = 8
assert PER_BANK * BANKS >= BLOCKS
NG = 4
LOG2 = float(np.log(2.0))
CAP = 30.0
EPS = 1e-5


def build(nc, xT, xb, src, dst, weight, fT, bond, w_in, b_in, w_f1, b_f1, w_f2, b_f2, w_o1, b_o1, w_o2, b_o2,
          W1, b1, W2, b2, out):
    h_rows = nc.dram_tensor("h_rows", (NPAD, FILT), F32).ap()
    v_rows = nc.dram_tensor("v_rows", (NPAD, HID), F32).ap()
    slots = nc.dram_tensor("slots", (SLOTS, REC), F32).ap()
    tile_table = nc.dram_tensor("tile_table", (2, P * TC), I32).ap()
    slot_steps = slots.rearrange("(g p t) c -> g p (t c)", p=P, t=STEP)

    with ExitStack() as ctx:
        def sb(name, shape, dt=F32):
            return ctx.enter_context(nc.sbuf_tensor(name, shape, dt))

        def sem(name):
            return ctx.enter_context(nc.semaphore(name))

        def sems(name, n=2):
            return [sem(f"{name}{k}") for k in range(n)]

        ps = ctx.enter_context(nc.psum_tensor("ps", [P, BANKS, 512], F32))

        zeros = sb("zeros", [P, STEP * REC])
        ident = sb("ident", [P, P])
        ones_bf = sb("ones_bf", [P, P], BF16)
        before = sb("before", [P, P], BF16)
        not_before = sb("not_before", [P, P], BF16)
        iota_b = sb("iota_b", [P, BLOCKS])
        iota_n = sb("iota_n", [P, NB])
        tile_no = sb("tile_no", [P, TC])
        lane = sb("lane", [P, 1])
        half = sb("half", [P, 1])
        w_in_s = sb("w_in_s", [P, FILT])
        b_in_s = sb("b_in_s", [P, FILT])
        wf1_s = sb("wf1_s", [RBF, FILT])
        bf1_s = sb("bf1_s", [P, 1])
        bf1_l = sb("bf1_l", [P, 1])
        wf2_s = sb("wf2_s", [P, FILT])
        bf2_s = sb("bf2_s", [P, FILT])
        wo1_s = sb("wo1_s", [P, HID])
        bo1_s = sb("bo1_s", [P, 1])
        bo1_l = sb("bo1_l", [P, 1])
        wo2_s = sb("wo2_s", [P, HID])
        bo2_s = sb("bo2_s", [P, HID])
        wab_s = sb("wab_s", [P, 2 * HID])
        b1_s = sb("b1_s", [P, HID])
        w2_s = sb("w2_s", [P, HID])
        b2_s = sb("b2_s", [P, HID])

        x_blk = sb("x_blk", [P, BLOCKS, HID])
        src_w = sb("src_w", [P, BLOCKS, HID])
        xT_s = src_w[:, :, :].rearrange("p b d -> p (b d)")[:, 0:NPAD]
        sum1 = sb("sum1", [P, BLOCKS, HID])
        h_s = sum1[:, :, :].rearrange("p b d -> p (b d)")[:, 0:NT * FILT].rearrange("p (t f) -> p t f", f=FILT)
        sum0 = sb("sum0", [P, BLOCKS, FILT])
        deg = sb("deg", [P, BLOCKS])
        src_1 = sum0[:, :, :].rearrange("p b f -> p (b f)")[:, 0:TILES]
        src_i = sum0[:, :, :].rearrange("p b f -> p (b f)")[:, TILES:2 * TILES].bitcast(I32)
        w_s = sb("w_s", [P, TILES])
        blk_f = sb("blk_f", [P, TILES])
        meta = sb("meta", [P, TILES, 2], I32)
        table = sb("table", [2, P * TC], I32)

        bond_s = sb("bond_s", [P, 2, STEP * BOND])
        z_s = sb("z_s", [P, 2, 512])
        e_s = sb("e_s", [P, 2, 512])
        sp_s = sb("sp_s", [P, 2, 512])
        wt = sb("wt", [P, STEP, FILT])
        oh_b = sb("oh_b", [P, 2, STEP, BLOCKS], BF16)
        rank_m = sb("rank_m", [P, STEP, BLOCKS])
        pos_f = sb("pos_f", [P, BLOCKS])
        pos_i = sb("pos_i", [P, BLOCKS], I32)
        bits = sb("bits", [P, 3, BLOCKS], I32)
        slot_i = sb("slot_i", [P, 2, STEP], I32)
        fill_i = sb("fill_i", [P, BLOCKS], I32)
        dst_r = sb("dst_r", [P, 2, STEP], I32)
        rec = sb("rec", [P, 2, STEP, REC])
        rec_meta = rec[:].bitcast(I32)[:, :, :, R_META:R_META + 2]
        cnt = sb("cnt", [P, STEP, BLOCKS])
        base = sb("base", [P, STEP, BLOCKS])
        turned = sb("turned", [P, 2, NG * NB])
        blkn = sb("blkn", [P, 8, BLOCKS])
        ntile_i = sb("ntile_i", [P, BLOCKS], I32)
        tabf = sb("tabf", [P, 3, TC])
        tabi = sb("tabi", [P, 3, TC], I32)
        oh_n = sb("oh_n", [P, 2, STEP, P])
        oh_t = sb("oh_t", [P, 2, 512])
        act_s = sb("act_s", [P, 2, 4, HID])
        vg = sb("vg", [P, 2, STEP, HID])
        stat = sb("stat", [P, 4, BLOCKS])
        dst_i = vg[:].rearrange("p u t d -> p (u t d)").bitcast(I32)[:, 0:TILES]
        fT_s = oh_n[0:RBF].rearrange("p u t d -> p u (t d)")
        hj = act_s[:].rearrange("p u t d -> p (u t d)").rearrange("p (u t f) -> p u t f", u=2, f=FILT)
        blk_i = oh_n[:].rearrange("p u t d -> p (u t d)").bitcast(I32)[:, 0:TILES]
        cmp = act_s[:].rearrange("p u t d -> p (u t d)")[:, 0:TC * BLOCKS].rearrange("p (c b) -> p c b", b=BLOCKS)

        block = ctx.enter_context(nc.Block())

        s_ld = {k: sem("ld_" + k) for k in ("xT", "w", "edges", "xb", "table")}
        s_const, s_pool_const = sem("consts_dve"), sem("consts_pool")
        N_W = 17

        h_psum, h_sbuf, h_stored = sem("h_psum"), sem("h_sbuf"), sem("h_stored")
        prep = sem("prep")
        oh_ready, oh_used = sem("oh_ready"), sem("oh_used")
        cnt_ready, bases = sem("cnt_ready"), sem("bases")
        fill_ready, tail_clear = sem("fill_ready"), sem("tail_clear")
        tab_ready, tab_stored = sem("tab_ready"), sem("tab_stored")
        ft_in, ft_used, bond_in, bond_used = sems("ft_in"), sem("ft_used"), sems("bond_in"), sem("bond_used")
        dst_ready, hj_in = sem("dst_ready"), sems("hj_in")
        z_ready, zc_ready, ex_ready, ln_ready = sem("z_ready"), sem("zc_ready"), sem("ex_ready"), sem("ln_ready")
        sp_ready, wt_ready = sem("sp_ready"), sem("wt_ready")
        rank_ready, rank_read = sem("rank_ready"), sem("rank_read")
        dve_sort = sem("dve_sort")
        slot_ready, rec_dve, rec_act = sem("slot_ready"), sem("rec_dve"), sem("rec_act")
        rec_out = sems("rec_out")
        held = sem("held")
        phase = {k: sem("end_" + k) for k in ("sort", "sum", "node", "edge")}
        rb_in, rb_used = sems("rb_in"), sem("rb_used")
        ohn_ready, sum_done, sum0_ready = sem("ohn_ready"), sem("sum_done"), sem("sum0_ready")
        xb_ready, sum1_clear = sem("xb_ready"), sem("sum1_clear")
        n = {k: sem("node_" + k) for k in ("T", "Tc", "z", "zc", "e", "l", "sp", "o", "xc", "sq", "dve", "var", "std",
                                           "x1", "T2", "T2c", "uv", "u", "v")}
        wc_in, v_out = sem("wc_in"), sems("v_out")
        rc_in, rc_used = sems("rc_in"), sem("rc_used")
        e = {k: sem("edge_" + k) for k in ("oh", "oh_used", "bond", "T", "Tc", "pre", "add", "silu", "agg", "acc", "vg_used")}
        vg_in = [sems(f"vg_in{u}_") for u in range(2)]
        f = {k: sem("last_" + k) for k in ("T", "Tc", "y", "xc", "sq", "dve", "var", "std", "out")}

        def end(eng, name):
            eng.drain().then_inc(phase[name], 1)

        def slot_rows(eng, done, n0, pos, tmp, res):
            eng.tensor_scalar(tmp[0], pos, -SE, None, ALU.bitwise_and).then_inc(done, 1)
            eng.tensor_scalar(tmp[1], pos, P - 1, 3, ALU.bitwise_and, ALU.logical_shift_left).then_inc(done, 1)
            eng.tensor_scalar(tmp[2], pos, 7, STEP - 1, ALU.logical_shift_right, ALU.bitwise_and).then_inc(done, 1)
            eng.wait_ge(done, n0 + 2)
            eng.tensor_tensor(tmp[1], tmp[0], tmp[1], ALU.bitwise_or).then_inc(done, 1)
            eng.wait_ge(done, n0 + 4)
            return eng.tensor_tensor(res, tmp[1], tmp[2], ALU.bitwise_or)

        @block.sync
        def _(sp):
            sp.dma_start(src_i, src).then_inc(s_ld["edges"], 16)
            sp.dma_start(dst_i, dst).then_inc(s_ld["edges"], 16)
            sp.dma_start(w_s[:], weight).then_inc(s_ld["edges"], 16)
            row = lambda v, n: v.rearrange("(a n) -> a n", a=1).broadcast_to([P, n])
            col = lambda v: v.rearrange("(n a) -> n a", a=1)
            loads = [(w_in_s[:], w_in), (b_in_s[:], row(b_in, FILT)), (wf1_s[:], w_f1),
                     (bf1_s[0:FILT], col(b_f1)), (bf1_s[FILT:P], col(b_f1)),
                     (wf2_s[0:FILT], w_f2), (wf2_s[FILT:P], w_f2), (bf2_s[:], row(b_f2, FILT)),
                     (wo1_s[0:FILT], w_o1), (wo1_s[FILT:P], w_o1), (bo1_s[:], col(b_o1)),
                     (wo2_s[:], w_o2), (bo2_s[:], row(b_o2, HID)), (b1_s[:], row(b1, HID)),
                     (wab_s[:, 0:HID], W1[0:HID]), (wab_s[:, HID:2 * HID], W1[HID:2 * HID]),
                     (w2_s[:], W2), (b2_s[:], row(b2, HID))]
            assert len(loads) == N_W + 1
            for to, of in loads:
                sp.dma_start(to, of).then_inc(s_ld["w"], 16)
            sp.dma_start(xT_s, xT).then_inc(s_ld["xT"], 16)
            sp.dma_start(x_blk[0:NB], xb).then_inc(s_ld["xb"], 16)
            sp.wait_ge(s_const, 1)
            for g in range(STEPS, SLOT_STEPS):
                sp.dma_start(slot_steps[g], zeros[:]).then_inc(tail_clear, 16)
            for g in range(NT // 7):
                sp.wait_ge(h_sbuf, g + 1)
                sp.dma_start(h_rows.rearrange("(t p) f -> p t f", p=P)[:, 7 * g:7 * g + 7],
                             h_s[:, 7 * g:7 * g + 7]).then_inc(h_stored, 16)
            sp.wait_ge(tab_ready, 1)
            for k in range(2):
                sp.dma_start(tile_table[k].rearrange("(p c) -> p c", c=TC), tabi[:, k]).then_inc(tab_stored, 16)
            sp.wait_ge(tab_stored, 32)
            sp.dma_start(table[:], tile_table).then_inc(s_ld["table"], 16)

            with sp.Fori(0, STEPS // 2) as i:
                for u in range(2):
                    sp.wait_ge(ft_used, i * 2 + u + 1)
                    sp.dma_start(fT_s[:, u], fT[bass.ds(i * 2 + u, 1)].rearrange("a r e -> (a r) e")).then_inc(
                        ft_in[u], 16)
                    sp.wait_ge(bond_used, i * 2 + u + 1)
                    sp.dma_start(bond_s[:, u], bond[bass.ds(i * 2 + u, 1)].rearrange("a p e -> (a p) e")).then_inc(
                        bond_in[u], 16)

            sp.wait_ge(phase["sort"], 4)
            with sp.Fori(0, SLOT_STEPS // 2) as i:
                for u in range(2):
                    sp.wait_ge(rb_used, i * 2 + u + 1)
                    sp.dma_start(rec[:, u], slot_steps[bass.ds(i * 2 + u, 1)].rearrange(
                        "a p (t c) -> (a p) t c", c=REC)).then_inc(rb_in[u], 16)

            sp.wait_ge(phase["sum"], 1)
            wc_rows = W1[2 * HID:2 * HID + BOND].rearrange("r (a d) -> r a d", a=1)
            sp.dma_start(src_w[NB:P], wc_rows.broadcast_to([BOND, BLOCKS, HID])).then_inc(wc_in, 16)
            for g in range(BLOCKS // NG):
                sp.wait_ge(n["v"], g + 1)
                sp.dma_start(v_rows[NG * g * NB:NG * (g + 1) * NB].rearrange("(k n) d -> n k d", n=NB),
                             vg[0:NB, g % 2, 0:NG]).then_inc(v_out[g % 2], 16)

            sp.wait_ge(phase["node"], 3)
            with sp.Fori(0, SLOT_STEPS // 2) as i:
                for u in range(2):
                    sp.wait_ge(rc_used, i * 2 + u + 1)
                    sp.dma_start(rec[:, u], slot_steps[bass.ds(i * 2 + u, 1)].rearrange(
                        "a p (t c) -> (a p) t c", c=REC)).then_inc(rc_in[u], 16)

            sp.wait_ge(f["out"], 1)
            full = NODES // NB
            sp.dma_start(out[0:full * NB].rearrange("(b n) d -> n b d", n=NB), x_blk[0:NB, 0:full]).then_inc(
                h_stored, 16)
            sp.dma_start(out[full * NB:NODES], x_blk[0:NODES - full * NB, full]).then_inc(h_stored, 16)
            sp.wait_ge(h_stored, 16 * (NT // 7 + 2))

        @block.gpsimd
        def _(pool):
            pool.iota(iota_b[:], [[1, BLOCKS]], base=0, channel_multiplier=0,
                      allow_small_or_imprecise_dtypes=True).then_inc(s_pool_const, 1)
            pool.iota(iota_n[:], [[1, NB]], base=1, channel_multiplier=0,
                      allow_small_or_imprecise_dtypes=True).then_inc(s_pool_const, 1)
            pool.iota(tile_no[:], [[1, TC]], base=0, channel_multiplier=TC,
                      allow_small_or_imprecise_dtypes=True).then_inc(s_pool_const, 1)
            pool.iota(lane[:], [[1, 1]], base=0, channel_multiplier=1,
                      allow_small_or_imprecise_dtypes=True).then_inc(s_pool_const, 1)
            pool.wait_ge(s_const, 6)
            pool.affine_select(out=before[:], in_=before[:], compare_op=ALU.is_gt, fill=0.0, base=0,
                               pattern=[[1, P]], channel_multiplier=-1).then_inc(s_pool_const, 1)
            pool.affine_select(out=not_before[:], in_=not_before[:], compare_op=ALU.is_ge, fill=0.0, base=0,
                               pattern=[[-1, P]], channel_multiplier=1).then_inc(s_pool_const, 1)
            pool.affine_select(out=ident[:], in_=ident[:], compare_op=ALU.not_equal, fill=1.0, base=0,
                               pattern=[[-1, P]], channel_multiplier=1).then_inc(s_pool_const, 1)

            pool.wait_ge(s_ld["xb"], 16)
            pool.wait_ge(s_ld["w"], 16 * (N_W + 1))
            pool.tensor_tensor(x_blk[0:NB], x_blk[0:NB], bo2_s[0:NB].unsqueeze(1).to_broadcast([NB, BLOCKS, HID]),
                               ALU.add).then_inc(xb_ready, 1)
            pool.wait_ge(tail_clear, 16 * (SLOT_STEPS - STEPS))
            pool.wait_ge(fill_ready, 1)
            pool.sem_inc(held)
            for b in range(BLOCKS):
                pool.indirect_dma_start(slots, bass.IndirectOffsetOnAxis(fill_i[:, b:b + 1], 0), zeros[:, 0:REC],
                                        None).then_inc(rec_out[b % 2], 16)
            for u in range(2):
                pool.wait_ge(rec_out[u], 16 * BLOCKS // 2)
            pool.wait_ge(h_stored, 16 * (NT // 7))
            pool.sem_inc(held)
            pool.memset(sum1[:], 0.0).then_inc(sum1_clear, 1)

            with pool.Fori(0, STEPS // 2) as i:
                for u in range(2):
                    pool.wait_ge(dst_ready, i * 2 + u + 1)
                    pool.sem_inc(held)
                    for t in range(STEP):
                        pool.indirect_dma_start(hj[:, u, t], None, h_rows,
                                                bass.IndirectOffsetOnAxis(dst_r[:, u, t:t + 1], 0)).then_inc(
                            hj_in[u], 16)
                    pool.wait_ge(slot_ready, i * 2 + u + 1)
                    pool.wait_ge(rec_act, i * 2 + u + 1)
                    pool.wait_ge(rec_dve, i * 2 + u + 1)
                    pool.sem_inc(held)
                    for t in range(STEP):
                        pool.indirect_dma_start(slots, bass.IndirectOffsetOnAxis(slot_i[:, u, t:t + 1], 0),
                                                rec[:, u, t], None).then_inc(rec_out[u], 16)
            for u in range(2):
                pool.wait_ge(rec_out[u], 16 * (BLOCKS // 2 + TILES // 2))
            end(pool, "sort")

            for u in range(2):
                pool.wait_ge(v_out[u], 16 * (BLOCKS // NG // 2))
            with pool.Fori(0, SLOT_STEPS // 2) as i:
                for u in range(2):
                    pool.wait_ge(rc_in[u], i * 16 + 16)
                    pool.wait_ge(e["vg_used"], i * 2 + u + 1)
                    pool.sem_inc(held)
                    for t in range(STEP):
                        pool.indirect_dma_start(vg[:, u, t], None, v_rows,
                                                bass.IndirectOffsetOnAxis(rec_meta[:, u, t, 1:2], 0)).then_inc(
                            vg_in[u][t // 4], 16)

        @block.scalar
        def _(act):
            act.sem_inc(bond_used, 2)
            act.preload_act_table_set("natural_log_exp_and_others")
            with act.Fori(0, STEPS // 2) as i:
                for u in range(2):
                    k = i * 2 + u + 1
                    act.wait_ge(zc_ready, k)
                    act.activation(e_s[:, u], z_s[:, u], ACT.Exp).then_inc(ex_ready, 1)
                    act.wait_ge(ex_ready, k)
                    act.activation(e_s[:, u], e_s[:, u], ACT.Ln, bias=half[:, 0:1], scale=0.5).then_inc(ln_ready, 1)
                    act.wait_ge(bond_in[u], i * 16 + 16)
                    act.wait_ge(rec_out[u], i * P + 16 * (BLOCKS // 2))
                    act.activation(rec[:, u, :, R_BOND:R_BOND + BOND],
                                   bond_s[:, u].rearrange("p (t c) -> p t c", c=BOND), ACT.Copy).then_inc(rec_act, 1)
                    act.wait_ge(rec_act, k)
                    act.sem_inc(bond_used, 1)
            end(act, "sort")

            G = BLOCKS // NG
            for g in range(G + 1):
                if g < G:
                    act.wait_ge(n["T"], g + 1)
                    act.activation(turned[:, g % 2, 0:2 * NB], ps[:, g % 2, 0:2 * NB], ACT.Copy).then_inc(n["Tc"], 1)
                    act.wait_ge(n["zc"], g + 1)
                    act.activation(e_s[:, g % 2, 0:NG * NB], z_s[:, g % 2, 0:NG * NB], ACT.Exp).then_inc(n["e"], 1)
                    act.wait_ge(n["e"], g + 1)
                    act.activation(e_s[:, g % 2, 0:NG * NB], e_s[:, g % 2, 0:NG * NB], ACT.Ln, bias=half[:, 0:1],
                                   scale=0.5).then_inc(n["l"], 1)
                if g >= 1:
                    act.wait_ge(n["xc"], g)
                    act.activation(act_s[0:NB, (g - 1) % 2], x_blk[0:NB, NG * (g - 1):NG * g],
                                   ACT.Square).then_inc(n["sq"], 1)
            act.wait_ge(n["var"], 1)
            act.activation(stat[0:NB, 2], stat[0:NB, 1], ACT.Sqrt).then_inc(n["std"], 1)
            for g in range(G):
                act.wait_ge(n["T2"], g + 1)
                act.activation(turned[:, g % 2], ps[:, 4 + g % 2, 0:NG * NB], ACT.Copy).then_inc(n["T2c"], 1)
                act.wait_ge(n["uv"], g + 1)
                if g >= 2:
                    act.wait_ge(v_out[g % 2], 16 * (g // 2))
                act.activation(vg[0:NB, g % 2, 0:NG], ps[0:NB, g % 2 * 2 + 1].rearrange("p (b d) -> p b d", d=HID),
                               ACT.Copy).then_inc(n["v"], 1)
            end(act, "node")

            act.wait_ge(phase["node"], 3)
            for u in range(2):
                act.wait_ge(v_out[u], 16 * (BLOCKS // NG // 2))
            with act.Fori(0, SLOT_STEPS // 2) as i:
                for u in range(2):
                    k = i * 2 + u + 1
                    act.wait_ge(rc_in[u], i * 16 + 16)
                    act.wait_ge(e["oh_used"], k)
                    act.activation(oh_n[:, u, :, NB:P], rec[:, u, :, R_BOND:R_BOND + BOND], ACT.Copy).then_inc(
                        e["bond"], 1)
                    for q in range(2):
                        act.wait_ge(e["T"], k * 2 + (q - 1))
                        act.activation(oh_t[:, q], ps[:, q], ACT.Copy).then_inc(e["Tc"], 1)
                    for q in range(2):
                        act.wait_ge(e["add"], k * 2 + (q - 1))
                        act.activation(act_s[:, q], vg[:, u, 4 * q:4 * q + 4], ACT.Silu).then_inc(e["silu"], 1)
                    act.wait_ge(e["silu"], k * 2)
                    act.sem_inc(e["vg_used"], 1)
            end(act, "edge")

            for g in range(G):
                act.wait_ge(f["T"], g + 1)
                act.activation(turned[:, g % 2], ps[:, g % 2, 0:NG * NB], ACT.Copy).then_inc(f["Tc"], 1)
                act.wait_ge(f["xc"], g + 1)
                act.activation(act_s[0:NB, g % 2], x_blk[0:NB, NG * g:NG * (g + 1)], ACT.Square).then_inc(f["sq"], 1)
            act.wait_ge(f["var"], 1)
            act.activation(stat[0:NB, 2], stat[0:NB, 1], ACT.Sqrt).then_inc(f["std"], 1)

        @block.tensor
        def _(pe):
            pe.sem_inc(ft_used, 2)
            pe.sem_inc(oh_used, 2)
            pe.sem_inc(rb_used, 2)
            pe.wait_ge(s_ld["w"], 16 * (N_W + 1))
            pe.wait_ge(s_ld["xT"], 16)
            for g in range(NT // 7):
                if g >= 2:
                    pe.wait_ge(h_sbuf, g - 1)
                for t in range(7):
                    nodes = slice((7 * g + t) * P, (7 * g + t + 1) * P)
                    mm = pe.matmul(ps[:, g % 2, t * FILT:(t + 1) * FILT], xT_s[:, nodes], w_in_s[:],
                                   start=True, stop=True)
                mm.then_inc(h_psum, 1)

            pe.wait_ge(s_const, 6)
            pe.wait_ge(s_pool_const, 7)
            counts = ps[:, 2, 0:STEP * BLOCKS]
            pe.matmul(counts, zeros[:, 0:P], zeros[:, 0:STEP * BLOCKS], start=True, stop=True)
            with pe.Fori(0, STEPS // 2) as i:
                for u in range(2):
                    pe.wait_ge(oh_ready, i * 2 + u + 1)
                    pe.matmul(counts, ones_bf[:], oh_b[:, u].rearrange("p t b -> p (t b)"), start=False, stop=True,
                              skip_group_check=True).then_inc(oh_used, 1)
            pe.wait_ge(oh_used, 2 + STEPS)
            pe.sem_inc(cnt_ready, 1)

            run = ps[:, 4, 0:STEP * BLOCKS]
            pe.wait_ge(bases, 1)
            pe.matmul(run, ident[:], base[:].rearrange("p t b -> p (t b)"), start=True, stop=True)
            with pe.Fori(0, STEPS // 2) as i:
                for u in range(2):
                    k = i * 2 + u + 1
                    pe.wait_ge(ft_in[u], i * 16 + 16)
                    pe.matmul(ps[0:FILT, u], wf1_s[:], fT_s[:, u, 0:512], start=True, stop=True)
                    pe.matmul(ps[FILT:P, u], wf1_s[:], fT_s[:, u, 512:SE], start=True, stop=True).then_inc(z_ready, 1)
                    pe.wait_ge(z_ready, k)
                    pe.sem_inc(ft_used, 1)
                    pe.wait_ge(oh_ready, k + STEPS)
                    pe.matmul(run, before[:], oh_b[:, u].rearrange("p t b -> p (t b)"), start=False, stop=True,
                              skip_group_check=True).then_inc(rank_ready, 1)
                    pe.wait_ge(rank_read, k)
                    pe.matmul(run, not_before[:], oh_b[:, u].rearrange("p t b -> p (t b)"), start=False, stop=True,
                              skip_group_check=True).then_inc(oh_used, 1)
                    pe.wait_ge(sp_ready, k)
                    for t in range(STEP):
                        half_ = slice(FILT * (t // 4), FILT * (t // 4) + FILT)
                        mm = pe.matmul(ps[:, 2 + 3 * u + t // 4, t % 4 * FILT:(t % 4 + 1) * FILT],
                                       sp_s[half_, u, (t % 4) * P:(t % 4 + 1) * P], wf2_s[half_, :],
                                       start=True, stop=True)
                    mm.then_inc(wt_ready, 1)
            end(pe, "sort")

            pe.wait_ge(s_ld["table"], 16)
            pe.wait_ge(phase["sort"], 4)
            for k in range(BANKS):
                pe.matmul(ps[:, k], zeros[:, 0:P], zeros[:, 0:512], start=True, stop=True)
            flat = ps[:].rearrange("p k n -> p (k n)")
            with pe.Fori(0, SLOT_STEPS // 2) as i:
                for u in range(2):
                    _, at = nc.values_load_multi_w_load_instructions(
                        table[1:2, bass.ds(i * (2 * STEP) + u * STEP, STEP)], PE_ONLY, min_val=0,
                        max_val=(BANKS - 1) * 512 + (PER_BANK - 1) * MSG,
                        skip_runtime_bounds_check_because="clamped to the last block when the table is made")
                    pe.wait_ge(rb_in[u], i * 16 + 16)
                    pe.wait_ge(ohn_ready, i * 2 + u + 1)
                    for t in range(STEP):
                        mm = pe.matmul(flat[0:NB, bass.ds(at[t], MSG)], oh_n[:, u, t, 0:NB], rec[:, u, t, 0:MSG],
                                       start=False, stop=True, skip_group_check=True)
                    mm.then_inc(rb_used, 1)
            pe.wait_ge(rb_used, 2 + SLOT_STEPS)
            pe.sem_inc(sum_done, 1)

            pe.wait_ge(sum0_ready, 1)
            G = BLOCKS // NG
            for g in range(G + 1):
                if g < G:
                    if g >= 2:
                        pe.wait_ge(n["Tc"], g - 1)
                    for q in range(2):
                        b = NG * g + 2 * q
                        mm = pe.transpose(ps[:, g % 2, q * NB:(q + 1) * NB],
                                          sum0[0:NB, b:b + 2].rearrange("p b f -> p (b f)"), ident[0:NB, 0:NB])
                    mm.then_inc(n["T"], 1)
                    pe.wait_ge(n["Tc"], g + 1)
                    for j in range(NG):
                        half_ = slice(FILT * (j % 2), FILT * (j % 2) + FILT)
                        mm = pe.matmul(ps[:, 2 + 4 * (g % 2) + j % 2, j // 2 * NB:(j // 2 + 1) * NB], wo1_s[half_, :],
                                       turned[half_, g % 2, j // 2 * NB:(j // 2 + 1) * NB], start=True, stop=True)
                    mm.then_inc(n["z"], 1)
                if g >= 1:
                    p = g - 1
                    pe.wait_ge(n["sp"], g)
                    if g >= 3:
                        pe.wait_ge(n["xc"], g - 2)
                    for j in range(NG):
                        at_ = j % 2 * (NG // 2) + j // 2
                        mm = pe.matmul(ps[0:NB, 4 + p % 2, j * HID:(j + 1) * HID],
                                       sp_s[:, p % 2, at_ * NB:(at_ + 1) * NB], wo2_s[:], start=True, stop=True)
                    mm.then_inc(n["o"], 1)
            for g in range(G):
                pe.wait_ge(n["x1"], g + 1)
                for j in range(NG):
                    mm = pe.transpose(ps[:, 4 + g % 2, j * NB:(j + 1) * NB], x_blk[0:NB, NG * g + j],
                                      ident[0:NB, 0:NB])
                mm.then_inc(n["T2"], 1)
                pe.wait_ge(n["T2c"], g + 1)
                if g >= 2:
                    pe.wait_ge(n["u"], g - 1)
                    pe.wait_ge(n["v"], g - 1)
                for j in range(NG):
                    for k in range(2):
                        mm = pe.matmul(ps[0:NB, g % 2 * 2 + k, j * HID:(j + 1) * HID],
                                       turned[:, g % 2, j * NB:(j + 1) * NB], wab_s[:, k * HID:(k + 1) * HID],
                                       start=True, stop=True)
                mm.then_inc(n["uv"], 1)
            end(pe, "node")

            pe.wait_ge(phase["node"], 3)
            pe.wait_ge(wc_in, 16)
            src_flat = src_w[:].rearrange("p b d -> p (b d)")
            with pe.Fori(0, SLOT_STEPS // 2) as i:
                for u in range(2):
                    k = i * 2 + u + 1
                    _, at = nc.values_load_multi_w_load_instructions(
                        table[0:1, bass.ds(i * (2 * STEP) + u * STEP, STEP)], PE_ONLY, min_val=0,
                        max_val=(BLOCKS - 1) * HID,
                        skip_runtime_bounds_check_because="clamped to the last block when the table is made")
                    pe.wait_ge(e["oh"], k)
                    pe.wait_ge(e["bond"], k)
                    for q in range(2):
                        for t in range(4):
                            mm = pe.transpose(ps[:, q, t * P:(t + 1) * P], oh_n[:, u, 4 * q + t], ident[:])
                        mm.then_inc(e["T"], 1)
                    for q in range(2):
                        pe.wait_ge(e["Tc"], k * 2 + (q - 1))
                        for t in range(4):
                            mm = pe.matmul(ps[:, 2 + q, t * HID:(t + 1) * HID], oh_t[:, q, t * P:(t + 1) * P],
                                           src_flat[:, bass.ds(at[4 * q + t], HID)], start=True, stop=True)
                        mm.then_inc(e["pre"], 1)
                    for q in range(2):
                        pe.wait_ge(e["silu"], k * 2 + (q - 1))
                        pe.wait_ge(e["acc"], (k * 2 + (q - 1)) * 4)
                        for t in range(4):
                            mm = pe.matmul(ps[0:NB, 4 + q, t * HID:(t + 1) * HID], oh_n[:, u, 4 * q + t, 0:NB],
                                           act_s[:, q, t], start=True, stop=True)
                        mm.then_inc(e["agg"], 1)
                    pe.wait_ge(e["agg"], k * 2)
                    pe.sem_inc(e["oh_used"], 1)
            end(pe, "edge")

            pe.wait_ge(phase["edge"], 3)
            for g in range(G):
                if g >= 2:
                    pe.wait_ge(f["Tc"], g - 1)
                for j in range(NG):
                    mm = pe.transpose(ps[:, g % 2, j * NB:(j + 1) * NB], sum1[0:NB, NG * g + j], ident[0:NB, 0:NB])
                mm.then_inc(f["T"], 1)
                pe.wait_ge(f["Tc"], g + 1)
                if g >= 2:
                    pe.wait_ge(f["xc"], g - 1)
                for j in range(NG):
                    mm = pe.matmul(ps[0:NB, 2 + g % 2, j * HID:(j + 1) * HID], turned[:, g % 2, j * NB:(j + 1) * NB],
                                   w2_s[:], start=True, stop=True)
                mm.then_inc(f["y"], 1)

        @block.vector
        def _(dve):
            for to, v in ((zeros, 0.0), (ones_bf, 1.0), (before, 1.0), (not_before, 1.0), (ident, 0.0), (half, 0.5),
                          (rec, 0.0)):
                dve.memset(to[:], v).then_inc(s_const, 1)
            dve.wait_ge(s_const, 7)
            dve.memset(rec[:, :, :, R_ONE:R_ONE + 1], 1.0).then_inc(s_const, 1)

            dve.wait_ge(s_ld["edges"], 48)
            dve.tensor_scalar(blk_i, src_i, 1.0 / NB, 0.5 / NB - 0.5, ALU.mult, ALU.add).then_inc(prep, 1)
            dve.tensor_scalar(src_1, src_i, 1.0, None, ALU.add).then_inc(prep, 1)
            dve.tensor_copy(meta[:, :, 1], dst_i).then_inc(prep, 1)
            dve.wait_ge(prep, 1)
            dve.tensor_copy(blk_f[:], blk_i).then_inc(prep, 1)
            dve.wait_ge(prep, 4)
            dve.scalar_tensor_tensor(out=meta[:, :, 0], in0=blk_f[:], scalar=-float(NB), in1=src_1, op0=ALU.mult,
                                     op1=ALU.add).then_inc(prep, 1)
            dve.wait_ge(s_ld["w"], 16 * (N_W + 1))
            dve.tensor_scalar(bf1_l[:], bf1_s[:], -LOG2, None, ALU.add).then_inc(prep, 1)
            dve.tensor_scalar(bo1_l[:], bo1_s[:], -LOG2, None, ALU.add).then_inc(prep, 1)

            for g in range(NT // 7):
                dve.wait_ge(h_psum, g + 1)
                dve.tensor_tensor(h_s[:, 7 * g:7 * g + 7], ps[:, g % 2, 0:7 * FILT].rearrange("p (t f) -> p t f", f=FILT),
                                  b_in_s[:].unsqueeze(1).to_broadcast([P, 7, FILT]), ALU.add).then_inc(h_sbuf, 1)

            def one_hot_block(k, u):
                return dve.tensor_tensor(oh_b[:, u], blk_f[:, bass.ds(k * STEP, STEP)].unsqueeze(2).to_broadcast(
                    [P, STEP, BLOCKS]), iota_b[:].unsqueeze(1).to_broadcast([P, STEP, BLOCKS]), ALU.is_equal)

            dve.wait_ge(s_pool_const, 7)
            dve.wait_ge(prep, 7)
            with dve.Fori(0, STEPS // 2) as i:
                for u in range(2):
                    dve.wait_ge(oh_used, i * 2 + u + 1)
                    one_hot_block(i * 2 + u, u).then_inc(oh_ready, 1)

            dve_n = [0]

            def link(ins, s=n["dve"]):
                dve_n[0] += 1
                ins.then_inc(s, 1)
                dve.wait_ge(s, dve_n[0])

            total, ntile, end_t, start_t, one, last_t, pos_b = (blkn[:, j] for j in range(7))
            dve.wait_ge(cnt_ready, 1)
            link(dve.tensor_copy(cnt[:], ps[:, 2, 0:STEP * BLOCKS].rearrange("p (t b) -> p t b", b=BLOCKS)))
            link(dve.tensor_reduce(total, cnt[:].rearrange("p t b -> p b t"), X, ALU.add))
            link(dve.tensor_scalar(ntile_i[:], total, 1.0 / P, (P - 1) / 2.0 / P, ALU.mult, ALU.add))
            link(dve.memset(one, 1.0))
            link(dve.tensor_copy(ntile, ntile_i[:]))
            link(dve.tensor_tensor_scan(end_t, one, ntile, 0.0, ALU.mult, ALU.add))
            link(dve.tensor_tensor(start_t, end_t, ntile, ALU.subtract))
            link(dve.tensor_scalar(base[:, 0], start_t, float(P), None, ALU.mult))
            for t in range(1, STEP):
                link(dve.tensor_tensor(base[:, t], base[:, t - 1], cnt[:, t - 1], ALU.add))
            dve.sem_inc(bases, 1)
            link(dve.tensor_scalar(last_t, end_t, -1.0, 0.0, ALU.add, ALU.max))
            link(dve.tensor_scalar(pos_b, last_t, float(P), lane[:, 0:1], ALU.mult, ALU.add))
            link(dve.tensor_copy(pos_i[:], pos_b))
            link(slot_rows(dve, prep, 7, pos_i[:], [bits[:, j] for j in range(3)], fill_i[:]))
            dve.sem_inc(fill_ready, 1)
            link(dve.tensor_tensor(cmp, tile_no[:].unsqueeze(2).to_broadcast([P, TC, BLOCKS]),
                                   end_t.unsqueeze(1).to_broadcast([P, TC, BLOCKS]), ALU.is_ge))
            link(dve.tensor_reduce(tabf[:, 0], cmp, X, ALU.add))
            link(dve.tensor_scalar(tabf[:, 0], tabf[:, 0], float(BLOCKS - 1), None, ALU.min))
            link(dve.tensor_scalar(tabi[:, 2], tabf[:, 0], 1.0 / PER_BANK, 0.5 / PER_BANK - 0.5, ALU.mult, ALU.add))
            link(dve.tensor_copy(tabf[:, 1], tabi[:, 2]))
            link(dve.tensor_scalar(tabf[:, 2], tabf[:, 0], float(MSG), None, ALU.mult))
            link(dve.tensor_scalar(tabi[:, 0], tabf[:, 0], float(HID), None, ALU.mult))
            link(dve.scalar_tensor_tensor(out=tabi[:, 1], in0=tabf[:, 1], scalar=float(512 - PER_BANK * MSG),
                                          in1=tabf[:, 2], op0=ALU.mult, op1=ALU.add))
            dve.sem_inc(tab_ready, 1)

            CH = 10
            with dve.Fori(0, STEPS // 2) as i:
                for u in range(2):
                    k = i * 2 + u + 1
                    done = (i * 2 + u) * CH
                    dve.tensor_copy(dst_r[:, u], meta[:, bass.ds((i * 2 + u) * STEP, STEP), 1]).then_inc(dst_ready, 1)
                    dve.wait_ge(z_ready, k)
                    dve.tensor_scalar(z_s[:, u], ps[:, u], bf1_s[:, 0:1], CAP, ALU.add, ALU.min).then_inc(zc_ready, 1)
                    dve.wait_ge(oh_used, k + STEPS)
                    one_hot_block(i * 2 + u, u).then_inc(oh_ready, 1)
                    dve.wait_ge(rank_ready, k)
                    dve.tensor_tensor(rank_m[:], ps[:, 4, 0:STEP * BLOCKS].rearrange("p (t b) -> p t b", b=BLOCKS),
                                      oh_b[:, u], ALU.mult).then_inc(rank_read, 1)
                    dve.wait_ge(rank_read, k)
                    dve.tensor_reduce(pos_f[:, 0:STEP], rank_m[:], X, ALU.add).then_inc(dve_sort, 1)
                    dve.wait_ge(dve_sort, done + 1)
                    dve.tensor_copy(pos_i[:, 0:STEP], pos_f[:, 0:STEP]).then_inc(dve_sort, 1)
                    dve.wait_ge(dve_sort, done + 2)
                    dve.wait_ge(rec_out[u], i * P + 16 * (BLOCKS // 2))
                    slot_rows(dve, dve_sort, done + 2, pos_i[:, 0:STEP], [bits[:, j, 0:STEP] for j in range(3)],
                              slot_i[:, u]).then_inc(slot_ready, 1)
                    dve.tensor_copy(rec_meta[:, u], meta[:, bass.ds((i * 2 + u) * STEP, STEP), :]).then_inc(dve_sort, 1)
                    dve.wait_ge(ln_ready, k)
                    dve.scalar_tensor_tensor(out=sp_s[:, u], in0=ps[:, u], scalar=bf1_l[:, 0:1], in1=e_s[:, u],
                                             op0=ALU.add, op1=ALU.max).then_inc(sp_ready, 1)
                    dve.wait_ge(wt_ready, k)
                    dve.tensor_tensor(wt[:].rearrange("p (a t) f -> p a t f", a=2),
                                      ps[:, 2 + 3 * u:4 + 3 * u, 0:4 * FILT].rearrange("p a (t f) -> p a t f", f=FILT),
                                      bf2_s[:].unsqueeze(1).unsqueeze(1).to_broadcast([P, 2, 4, FILT]),
                                      ALU.add).then_inc(dve_sort, 1)
                    dve.wait_ge(dve_sort, done + 8)
                    dve.tensor_tensor(wt[:], wt[:], w_s[:, bass.ds((i * 2 + u) * STEP, STEP)].unsqueeze(2).to_broadcast(
                        [P, STEP, FILT]), ALU.mult).then_inc(dve_sort, 1)
                    dve.wait_ge(dve_sort, done + 9)
                    dve.wait_ge(hj_in[u], i * P + P)
                    dve.tensor_tensor(rec[:, u, :, 0:FILT], wt[:], hj[:, u], ALU.mult).then_inc(dve_sort, 1)
                    dve.wait_ge(dve_sort, done + CH)
                    dve.sem_inc(rec_dve, 1)
            end(dve, "sort")

            def one_hot_node(u):
                return dve.tensor_tensor(oh_n[:, u, :, 0:NB], rec_meta[:, u, :, 0:1].to_broadcast([P, STEP, NB]),
                                         iota_n[:].unsqueeze(1).to_broadcast([P, STEP, NB]), ALU.is_equal)

            with dve.Fori(0, SLOT_STEPS // 2) as i:
                for u in range(2):
                    dve.wait_ge(rb_in[u], i * 16 + 16)
                    dve.wait_ge(rb_used, i * 2 + u + 1)
                    one_hot_node(u).then_inc(ohn_ready, 1)
            dve.wait_ge(sum_done, 1)
            for k in range(BANKS):
                sums = ps[0:NB, k, 0:PER_BANK * MSG].rearrange("p (b f) -> p b f", f=MSG)
                dve.tensor_copy(sum0[0:NB, PER_BANK * k:PER_BANK * (k + 1)], sums[:, :, 0:FILT])
                last = dve.tensor_copy(deg[0:NB, PER_BANK * k:PER_BANK * (k + 1)], sums[:, :, FILT])
            last.then_inc(sum0_ready, 1)
            end(dve, "sum")

            G = BLOCKS // NG
            dve.wait_ge(xb_ready, 1)

            def centre(g, s, into):
                blocks = slice(NG * g, NG * (g + 1))
                link(dve.tensor_reduce(stat[0:NB, 0, blocks], x_blk[0:NB, blocks], X, ALU.add), s)
                link(dve.tensor_scalar(stat[0:NB, 0, blocks], stat[0:NB, 0, blocks], -1.0 / HID, None, ALU.mult), s)
                dve.tensor_tensor(x_blk[0:NB, blocks], x_blk[0:NB, blocks],
                                  stat[0:NB, 0, blocks].unsqueeze(2).to_broadcast([NB, NG, HID]),
                                  ALU.add).then_inc(into, 1)

            def square_sum(g, sq):
                dve.wait_ge(sq, g + 1)
                return dve.tensor_reduce(stat[0:NB, 1, NG * g:NG * (g + 1)], act_s[0:NB, g % 2], X, ALU.add)

            for g in range(G + 1):
                if g < G:
                    dve.wait_ge(n["z"], g + 1)
                    z = ps[:, 2 + 4 * (g % 2):4 + 4 * (g % 2), 0:2 * NB]
                    both = lambda v: v[:, g % 2, 0:NG * NB].rearrange("p (a n) -> p a n", a=2)
                    dve.tensor_scalar(both(z_s), z, bo1_s[:, 0:1], CAP, ALU.add, ALU.min).then_inc(n["zc"], 1)
                    dve.wait_ge(n["l"], g + 1)
                    dve.scalar_tensor_tensor(out=both(sp_s), in0=z, scalar=bo1_l[:, 0:1], in1=both(e_s), op0=ALU.add,
                                             op1=ALU.max).then_inc(n["sp"], 1)
                if g >= 1:
                    p = g - 1
                    dve.wait_ge(n["o"], g)
                    link(dve.tensor_tensor(x_blk[0:NB, NG * p:NG * g], x_blk[0:NB, NG * p:NG * g],
                                           ps[0:NB, 4 + p % 2].rearrange("p (b d) -> p b d", d=HID), ALU.add))
                    centre(p, n["dve"], n["xc"])
                    link(square_sum(p, n["sq"]))

            def deviation(s, var, std):
                dve.tensor_scalar(stat[0:NB, 1], stat[0:NB, 1], 1.0 / HID, EPS, ALU.mult, ALU.add).then_inc(var, 1)
                dve.wait_ge(std, 1)
                link(dve.reciprocal(stat[0:NB, 3], stat[0:NB, 2]), s)

            def scale(g):
                blocks = slice(NG * g, NG * (g + 1))
                return dve.tensor_tensor(x_blk[0:NB, blocks], x_blk[0:NB, blocks],
                                         stat[0:NB, 3, blocks].unsqueeze(2).to_broadcast([NB, NG, HID]), ALU.mult)

            deviation(n["dve"], n["var"], n["std"])
            for g in range(G + 1):
                if g < G:
                    scale(g).then_inc(n["x1"], 1)
                if g >= 1:
                    p = g - 1
                    dve.wait_ge(n["uv"], g)
                    dve.tensor_tensor(src_w[0:NB, NG * p:NG * g], ps[0:NB, p % 2 * 2].rearrange("p (b d) -> p b d", d=HID),
                                      b1_s[0:NB].unsqueeze(1).to_broadcast([NB, NG, HID]), ALU.add).then_inc(n["u"], 1)
            end(dve, "node")

            dve.wait_ge(phase["node"], 3)
            dve.wait_ge(sum1_clear, 1)
            dve.sem_inc(rc_used, 2)
            dve.sem_inc(e["oh_used"], 2)
            dve.sem_inc(e["vg_used"], 2)
            dve.sem_inc(e["acc"], 8)
            sum_flat = sum1[:].rearrange("p b d -> p (b d)")
            with dve.Fori(0, SLOT_STEPS // 2) as i:
                for u in range(2):
                    k = i * 2 + u + 1
                    _, at = nc.values_load_multi_w_load_instructions(
                        table[0:1, bass.ds(i * (2 * STEP) + u * STEP, STEP)], DVE_ONLY, min_val=0,
                        max_val=(BLOCKS - 1) * HID,
                        skip_runtime_bounds_check_because="clamped to the last block when the table is made")
                    dve.wait_ge(rc_in[u], i * 16 + 16)
                    dve.wait_ge(e["oh_used"], k)
                    one_hot_node(u).then_inc(e["oh"], 1)
                    for q in range(2):
                        dve.wait_ge(vg_in[u][q], i * 64 + 64)
                        dve.wait_ge(e["pre"], k * 2 + (q - 1))
                        rows = vg[:, u, 4 * q:4 * q + 4]
                        dve.tensor_tensor(rows, rows, ps[:, 2 + q].rearrange("p (t d) -> p t d", d=HID),
                                          ALU.add).then_inc(e["add"], 1)
                    dve.wait_ge(e["bond"], k)
                    dve.sem_inc(rc_used, 1)
                    for q in range(2):
                        dve.wait_ge(e["agg"], k * 2 + (q - 1))
                        for t in range(4):
                            dve.wait_ge(e["acc"], (k * 2 + (q - 1)) * 4 + (4 + t))
                            here = sum_flat[0:NB, bass.ds(at[4 * q + t], HID)]
                            dve.tensor_tensor(here, here, ps[0:NB, 4 + q, t * HID:(t + 1) * HID], ALU.add).then_inc(
                                e["acc"], 1)
            end(dve, "edge")

            dve_n[0] = 0
            for g in range(G):
                dve.wait_ge(f["y"], g + 1)
                blocks = slice(NG * g, NG * (g + 1))
                link(dve.tensor_tensor(x_blk[0:NB, blocks], x_blk[0:NB, blocks],
                                       ps[0:NB, 2 + g % 2].rearrange("p (b d) -> p b d", d=HID), ALU.add), f["dve"])
                for b in range(NG * g, NG * (g + 1)):
                    ins = dve.scalar_tensor_tensor(out=x_blk[0:NB, b], in0=b2_s[0:NB], scalar=deg[0:NB, b:b + 1],
                                                   in1=x_blk[0:NB, b], op0=ALU.mult, op1=ALU.add)
                link(ins, f["dve"])
                centre(g, f["dve"], f["xc"])
                link(square_sum(g, f["sq"]), f["dve"])
            deviation(f["dve"], f["var"], f["std"])
            for g in range(G):
                ins = scale(g)
            ins.then_inc(f["out"], 1)


_OUT = ((NODES, HID), np.float32)


def kernel(**inputs):
    import concourse.bacc as bacc
    from concourse.bass_utils import run_bass_kernel_spmd

    a = {k: np.asarray(v) for k, v in inputs.items()}

    def edges(v, fill):
        rest = np.full((PADDED - EDGES,) + v.shape[1:], fill, v.dtype)
        return np.concatenate([v, rest])

    def by_tile(v, fill):
        return np.ascontiguousarray(edges(v, fill).reshape(TILES, P).T)

    x = np.concatenate([a["x"], np.zeros((NPAD - NODES, HID), np.float32)])
    laid = {
        "xT": np.ascontiguousarray(x.T),
        "xb": np.ascontiguousarray(x.reshape(BLOCKS, NB, HID).transpose(1, 0, 2)),
        "src": by_tile(a["src"], NODES),
        "dst": by_tile(a["dst"], 0),
        "weight": by_tile(a["edge_weight"], 0),
        "fT": np.ascontiguousarray(edges(a["edge_attr_32"], 0).reshape(STEPS, SE, RBF).transpose(0, 2, 1)),
        "bond": np.ascontiguousarray(edges(a["edge_attr_16"], 0).reshape(STEPS, STEP, P, BOND).transpose(
            0, 2, 1, 3).reshape(STEPS, P, STEP * BOND)),
    }
    for name in ("w_in", "b_in", "w_f1", "b_f1", "w_f2", "b_f2", "w_o1", "b_o1", "w_o2", "b_o2"):
        laid[name] = np.ascontiguousarray(a["L0_gnn_" + name])
    for name in ("W1", "b1", "W2", "b2"):
        laid[name] = np.ascontiguousarray(a["L1_gnn_" + name])
    nc = bacc.Bacc("TRN2", target_bir_lowering=False, num_devices=1)
    args = {k: nc.dram_tensor("in_" + k, v.shape, mybir.dt.from_np(v.dtype), kind="ExternalInput").ap()
            for k, v in laid.items()}
    out = nc.dram_tensor("out", _OUT[0], F32, kind="ExternalOutput").ap()
    build(nc, out=out, **args)
    r = run_bass_kernel_spmd(nc, [{"in_" + k: v for k, v in laid.items()}], core_ids=[0])
    return r.results[0]["out"]
```

```python
from contextlib import ExitStack

import numpy as np

import concourse.bass as bass
from concourse import mybir

ALU = mybir.AluOpType
ACT = mybir.ActivationFunctionType
F32 = mybir.dt.float32
I32 = mybir.dt.int32
BF16 = mybir.dt.bfloat16
X = mybir.AxisListType.X
PE_ONLY = (mybir.EngineType.PE,)
DVE_ONLY = (mybir.EngineType.DVE,)

P = 128
NODES, HID, FILT, RBF, BOND = 6250, 128, 64, 32, 16
EDGES = 206250
NB = HID - BOND
BLOCKS = -(-NODES // NB)
STEP = 8
SE = STEP * P
TILES = -(-EDGES // (2 * SE)) * 2 * STEP
STEPS = TILES // STEP
PADDED = TILES * P
SLOT_TILES = -(-(TILES + BLOCKS) // (2 * STEP)) * 2 * STEP
SLOT_STEPS = SLOT_TILES // STEP
SLOTS = SLOT_TILES * P
TC = -(-SLOT_TILES // P)
MSG = FILT + 1
WIDE = 96
REC = P
R_ONE, R_BOND, R_META = FILT, WIDE, WIDE + BOND
WIN = 64
NPAD = BLOCKS * NB
NT = NPAD // P
assert NPAD == NT * P and TILES * P == PADDED
PER_BANK = 512 // MSG
BANKS = 8
assert PER_BANK * BANKS >= BLOCKS and (PER_BANK - 1) * MSG + WIDE <= 512
NG = 4
LOG2 = float(np.log(2.0))
CAP = 30.0
EPS = 1e-5


def build(nc, xT, xb, src, dst, dst_steps, weight, fT, bond, w_in, b_in, w_f1, b_f1, w_f2, b_f2, w_o1, b_o1, w_o2, b_o2,
          W1, b1, W2, b2, out):
    h_rows = nc.dram_tensor("h_rows", (NPAD, FILT), F32).ap()
    v_rows = nc.dram_tensor("v_rows", (NPAD, HID), F32).ap()
    slots = nc.dram_tensor("slots", (SLOTS, REC), F32).ap()
    rel_rows = nc.dram_tensor("rel_rows", (STEPS, SE), BF16).ap()
    win_table = nc.dram_tensor("win_table", (2, STEPS), I32).ap()
    tile_table = nc.dram_tensor("tile_table", (2, P * TC), I32).ap()
    slot_steps = slots.rearrange("(g p t) c -> g p (t c)", p=P, t=STEP)

    with ExitStack() as ctx:
        def sb(name, shape, dt=F32):
            return ctx.enter_context(nc.sbuf_tensor(name, shape, dt))

        def sem(name):
            return ctx.enter_context(nc.semaphore(name))

        def sems(name, n=2):
            return [sem(f"{name}{k}") for k in range(n)]

        ps = ctx.enter_context(nc.psum_tensor("ps", [P, BANKS, 512], F32))

        zeros = sb("zeros", [P, STEP * REC])
        one_row = sb("one_row", [1, P])
        ident = sb("ident", [P, P])
        ones_bf = sb("ones_bf", [P, P], BF16)
        before = sb("before", [P, P], BF16)
        not_before = sb("not_before", [P, P], BF16)
        iota_b = sb("iota_b", [P, BLOCKS])
        iota_n = sb("iota_n", [P, NB])
        tile_no = sb("tile_no", [P, TC])
        lane = sb("lane", [P, 1])
        half = sb("half", [P, 1])
        lane_half = sb("lane_half", [P, 1])
        w_in_s = sb("w_in_s", [P, FILT])
        b_in_s = sb("b_in_s", [P, FILT])
        wf1_s = sb("wf1_s", [RBF, FILT])
        bf1_s = sb("bf1_s", [P, 1])
        bf1_l = sb("bf1_l", [P, 1])
        wf2_s = sb("wf2_s", [P, P])
        bf2_s = sb("bf2_s", [1, STEP * FILT])
        wo1_s = sb("wo1_s", [P, HID])
        bo1_s = sb("bo1_s", [P, 1])
        bo1_l = sb("bo1_l", [P, 1])
        wo2_s = sb("wo2_s", [P, HID])
        bo2_s = sb("bo2_s", [P, HID])
        wab_s = sb("wab_s", [P, 2 * HID])
        b1_s = sb("b1_s", [P, HID])
        w2_s = sb("w2_s", [P, HID])
        b2_s = sb("b2_s", [P, HID])

        x_blk = sb("x_blk", [P, BLOCKS, HID])
        src_w = sb("src_w", [P, BLOCKS, HID])
        xT_s = src_w[:, :, :].rearrange("p b d -> p (b d)")[:, 0:NPAD]
        sum1 = sb("sum1", [P, BLOCKS, HID])
        h_s = sum1[:, :, :].rearrange("p b d -> p (b d)")[:, 0:NT * FILT].rearrange("p (t f) -> p t f", f=FILT)
        sum0 = sb("sum0", [P, BLOCKS, FILT])
        deg = sb("deg", [P, BLOCKS])
        src_1 = sum0[:, :, :].rearrange("p b f -> p (b f)")[:, 0:TILES]
        src_i = sum0[:, :, :].rearrange("p b f -> p (b f)")[:, TILES:2 * TILES].bitcast(I32)
        w_s = sb("w_s", [P, TILES])
        blk_f = sb("blk_f", [P, TILES])
        meta = sb("meta", [P, TILES, 2], I32)
        table = sb("table", [2, P * TC], I32)
        spare = sum1[:, :, :].rearrange("p b d -> p (b d)")[0:STEPS // 2, NT * FILT:]
        dst_2 = spare[:, 0:2 * SE].bitcast(I32).rearrange("p (s e) -> p s e", e=SE)
        rel_2 = spare[:, 2 * SE:3 * SE].bitcast(BF16).rearrange("p (s e) -> p s e", e=SE)
        win_f = sb("win_f", [STEPS // 2, 3, 2])
        win_i = sb("win_i", [STEPS // 2, 2, 2], I32)
        win_s = sb("win_s", [1, 2, STEPS], I32)
        reach = sb("reach", [1, 1])
        is_local = sb("is_local", [1, 1], I32)

        bond_s = sb("bond_s", [P, 2, STEP * BOND])
        z_s = sb("z_s", [P, 2, 512])
        e_s = sb("e_s", [P, 2, 512])
        sp_s = sb("sp_s", [P, 2, 512])
        wt = sb("wt", [P, STEP, FILT])
        rel_s = sb("rel_s", [P, 2, SE // 2], BF16)
        h_win = sb("h_win", [P, 2, P])
        oh_b = sb("oh_b", [P, 2, STEP, BLOCKS], BF16)
        rank_m = sb("rank_m", [P, STEP, BLOCKS])
        pos_f = sb("pos_f", [P, BLOCKS])
        pos_i = sb("pos_i", [P, BLOCKS], I32)
        bits = sb("bits", [P, 3, BLOCKS], I32)
        slot_n = sb("slot_n", [P, 2, STEP], I32)
        slot_i = sb("slot_i", [P, 2, STEP], I32)
        fill_i = sb("fill_i", [P, BLOCKS], I32)
        dst_r = sb("dst_r", [P, 2, STEP], I32)
        rec = sb("rec", [P, 2, STEP, REC])
        rec_meta = rec[:].bitcast(I32)[:, :, :, R_META:R_META + 2]
        cnt = rank_m
        base = sb("base", [P, STEP, BLOCKS])
        blkn = sb("blkn", [P, 8, BLOCKS])
        ntile_i = sb("ntile_i", [P, BLOCKS], I32)
        tabf = sb("tabf", [P, 3, TC])
        tabi = sb("tabi", [P, 3, TC], I32)
        oh_n = sb("oh_n", [P, 2, STEP, P])
        oh_t = sb("oh_t", [P, 2, 512])
        act_s = sb("act_s", [P, 2, 4, HID])
        vg = sb("vg", [P, 2, STEP, HID])
        stat = sb("stat", [P, 4, BLOCKS])
        turned = oh_t[:].rearrange("p u n -> p (u n)")[:, 0:2 * NG * NB].rearrange("p (u n) -> p u n", u=2)
        dst_i = vg[:].rearrange("p u t d -> p (u t d)").bitcast(I32)[:, 0:TILES]
        on_dst = oh_t
        fT_s = oh_n[0:RBF].rearrange("p u t d -> p u (t d)")
        hj = act_s[:].rearrange("p u t d -> p (u t d)").rearrange("p (u t f) -> p u t f", u=2, f=FILT)
        sum_rec = [rec[:, 0], rec[:, 1], vg[:, 0]]
        sum_oh = [oh_n[:, 0], oh_n[:, 1], act_s[:].rearrange("p u t d -> p (u t) d")]
        blk_i = oh_n[:].rearrange("p u t d -> p (u t d)").bitcast(I32)[:, 0:TILES]
        cmp = act_s[:].rearrange("p u t d -> p (u t d)")[:, 0:TC * BLOCKS].rearrange("p (c b) -> p c b", b=BLOCKS)

        block = ctx.enter_context(nc.Block())

        s_ld = {k: sem("ld_" + k) for k in ("xT", "w", "edges", "xb", "table", "dst_2", "win")}
        WEIGHTS = 18
        s_const, s_pool_const = sem("consts_dve"), sem("consts_pool")

        h_psum, h_sbuf, h_stored = sem("h_psum"), sem("h_sbuf"), sem("h_stored")
        prep = sem("prep")
        oh_ready, oh_used = sem("oh_ready"), sem("oh_used")
        cnt_ready, bases = sem("cnt_ready"), sem("bases")
        fill_ready, tail_clear = sem("fill_ready"), sem("tail_clear")
        tab_ready, tab_stored = sem("tab_ready"), sem("tab_stored")
        ft_in, ft_used, bond_in, bond_used = sems("ft_in"), sem("ft_used"), sems("bond_in"), sem("bond_used")
        dst_ready, hj_in = sem("dst_ready"), sems("hj_in")
        z_ready, zc_ready, ex_ready, ln_ready = sem("z_ready"), sem("zc_ready"), sem("ex_ready"), sem("ln_ready")
        sp_ready, wt_ready = sem("sp_ready"), sem("wt_ready")
        rank_ready, rank_read = sem("rank_ready"), sem("rank_read")
        dve_slot, dve_rec = sem("dve_slot"), sem("dve_rec")
        win_part, win_ready, rel_stored, path_ready = sem("win_part"), sem("win_ready"), sem("rel_stored"), sem("path_ready")
        rel_in, win_in, on_dst_ready, hj_psum = sems("rel_in"), sems("win_in"), sem("on_dst_ready"), sem("hj_psum")
        slot_ready, rec_dve, rec_act = sem("slot_ready"), sem("rec_dve"), sem("rec_act")
        rec_out = sems("rec_out")
        held = sem("held")
        phase = {k: sem("end_" + k) for k in ("sort", "sum", "node", "edge")}
        rb_in, rb_used = sems("rb_in", 3), sem("rb_used")
        ohn_ready, sum_done, sum0_ready = sem("ohn_ready"), sem("sum_done"), sem("sum0_ready")
        xb_ready, sum1_clear = sem("xb_ready"), sem("sum1_clear")
        n = {k: sem("node_" + k) for k in ("T", "Tc", "z", "zc", "e", "l", "sp", "o", "xc", "sq", "dve", "var", "std",
                                           "x1", "T2", "T2c", "uv", "u", "v")}
        wc_in, v_out = sem("wc_in"), sems("v_out")
        rc_in, rc_used = sems("rc_in"), sem("rc_used")
        e = {k: sem("edge_" + k) for k in ("oh", "oh_used", "bond", "T", "Tc", "pre", "add", "silu", "agg", "acc",
                                           "vg_used")}
        vg_in = [sems(f"vg_in{u}_") for u in range(2)]
        f = {k: sem("last_" + k) for k in ("T", "Tc", "y", "xc", "sq", "dve", "var", "std", "out")}

        def sort_path(eng, loop):
            eng.wait_ge(path_ready, 1)
            near = eng.value_load(is_local[0:1, 0:1], min_val=0, max_val=1)
            with eng.If(near == 1):
                loop(True)
            with eng.Else():
                loop(False)

        def pairs(eng, steps, first, step):
            first()
            with eng.Fori(0, steps // 2 - 1) as i:
                for u in range(2):
                    step(i * 2 + u, i, u, True)
            step(steps - 2, steps // 2 - 1, 0, True)
            step(steps - 1, steps // 2 - 1, 1, False)

        def after(r, u):
            return (r + u, 1 - u)

        def end(eng, name):
            eng.drain().then_inc(phase[name], 1)

        def slot_rows(eng, done, n0, pos, tmp, res):
            eng.tensor_scalar(tmp[0], pos, -SE, None, ALU.bitwise_and).then_inc(done, 1)
            eng.tensor_scalar(tmp[1], pos, P - 1, 3, ALU.bitwise_and, ALU.logical_shift_left).then_inc(done, 1)
            eng.tensor_scalar(tmp[2], pos, 7, STEP - 1, ALU.logical_shift_right, ALU.bitwise_and).then_inc(done, 1)
            eng.wait_ge(done, n0 + 2)
            eng.tensor_tensor(tmp[1], tmp[0], tmp[1], ALU.bitwise_or).then_inc(done, 1)
            eng.wait_ge(done, n0 + 4)
            return eng.tensor_tensor(res, tmp[1], tmp[2], ALU.bitwise_or)

        @block.sync
        def _(sp):
            sp.dma_start(src_i, src).then_inc(s_ld["edges"], 16)
            sp.dma_start(dst_i, dst).then_inc(s_ld["edges"], 16)
            sp.dma_start(w_s[:], weight).then_inc(s_ld["edges"], 16)
            row = lambda v, n: v.rearrange("(a n) -> a n", a=1).broadcast_to([P, n])
            col = lambda v: v.rearrange("(n a) -> n a", a=1)
            loads = [(w_in_s[:], w_in), (b_in_s[:], row(b_in, FILT)), (wf1_s[:], w_f1),
                     (bf1_s[0:FILT], col(b_f1)), (bf1_s[FILT:P], col(b_f1)),
                     (wf2_s[0:FILT, 0:FILT], w_f2), (wf2_s[FILT:P, FILT:P], w_f2),
                     (bf2_s[:].rearrange("a (t f) -> a t f", f=FILT),
                      b_f2.rearrange("(a t f) -> a t f", a=1, t=1).broadcast_to([1, STEP, FILT])),
                     (wo1_s[0:FILT], w_o1), (wo1_s[FILT:P], w_o1), (bo1_s[:], col(b_o1)),
                     (wo2_s[:], w_o2), (bo2_s[:], row(b_o2, HID)), (b1_s[:], row(b1, HID)),
                     (wab_s[:, 0:HID], W1[0:HID]), (wab_s[:, HID:2 * HID], W1[HID:2 * HID]),
                     (w2_s[:], W2), (b2_s[:], row(b2, HID))]
            assert len(loads) == WEIGHTS
            sp.wait_ge(s_const, 3)
            for to, of in loads:
                sp.dma_start(to, of).then_inc(s_ld["w"], 16)
            sp.dma_start(xT_s, xT).then_inc(s_ld["xT"], 16)
            sp.dma_start(dst_2, dst_steps.rearrange("(p s) e -> p s e", s=2)).then_inc(s_ld["dst_2"], 16)
            sp.dma_start(x_blk[0:NB], xb).then_inc(s_ld["xb"], 16)
            for g in range(STEPS, SLOT_STEPS):
                sp.dma_start(slot_steps[g], zeros[:]).then_inc(tail_clear, 16)
            for g in range(NT // 7):
                sp.wait_ge(h_sbuf, g + 1)
                sp.dma_start(h_rows.rearrange("(t p) f -> p t f", p=P)[:, 7 * g:7 * g + 7],
                             h_s[:, 7 * g:7 * g + 7]).then_inc(h_stored, 16)
            sp.wait_ge(tab_ready, 1)
            for k in range(2):
                sp.dma_start(tile_table[k].rearrange("(p c) -> p c", c=TC), tabi[:, k]).then_inc(tab_stored, 16)
            sp.wait_ge(tab_stored, 32)
            sp.dma_start(table[:], tile_table).then_inc(s_ld["table"], 16)

            def sort_loads(local):
                def step(k, r, u):
                    sp.wait_ge(ft_used, k + 1)
                    sp.dma_start(fT_s[:, u], fT[bass.ds(k, 1)].rearrange("a r e -> (a r) e")).then_inc(ft_in[u], 16)
                    if local:
                        at = sp.value_load(win_s[0:1, 0, bass.ds(k, 1)], min_val=0, max_val=NPAD - WIN)
                        sp.wait_ge(on_dst_ready, k + 1)
                        for a in range(2):
                            sp.dma_start(rel_s[a * WIN:(a + 1) * WIN, u], rel_rows[
                                bass.ds(k, 1), a * (SE // 2):(a + 1) * (SE // 2)].broadcast_to(
                                [WIN, SE // 2])).then_inc(rel_in[u], 16)
                        sp.wait_ge(hj_psum, k + 1)
                        for a in range(2):
                            sp.dma_start(h_win[a * WIN:(a + 1) * WIN, u, a * FILT:(a + 1) * FILT],
                                         h_rows[bass.ds(at, WIN)]).then_inc(win_in[u], 16)
                    sp.wait_ge(bond_used, k + 1)
                    sp.dma_start(bond_s[:, u], bond[bass.ds(k, 1)].rearrange("a p e -> (a p) e")).then_inc(
                        bond_in[u], 16)

                with sp.Fori(0, STEPS // 2) as i:
                    for u in range(2):
                        step(i * 2 + u, i, u)

            sp.wait_ge(win_ready, 1)
            sp.dma_start(rel_rows.rearrange("(p s) e -> p s e", s=2), rel_2).then_inc(rel_stored, 16)
            for k in range(2):
                sp.dma_start(win_table[k].rearrange("(p s) -> p s", s=2), win_i[:, k]).then_inc(rel_stored, 16)
            sp.wait_ge(rel_stored, 48)
            sp.dma_start(win_s[:], win_table.rearrange("(a k) s -> a k s", a=1)).then_inc(s_ld["win"], 16)
            sp.wait_ge(h_stored, 16 * (NT // 7))
            sort_path(sp, sort_loads)

            sp.wait_ge(phase["sort"], 4)
            with sp.Fori(0, SLOT_STEPS // 3) as i:
                for u in range(3):
                    sp.wait_ge(rb_used, i * 3 + u + 1)
                    sp.dma_start(sum_rec[u], slot_steps[bass.ds(i * 3 + u, 1)].rearrange(
                        "a p (t c) -> (a p) t c", c=REC)).then_inc(rb_in[u], 16)

            sp.wait_ge(phase["sum"], 1)
            wc_rows = W1[2 * HID:2 * HID + BOND].rearrange("r (a d) -> r a d", a=1)
            sp.dma_start(src_w[NB:P], wc_rows.broadcast_to([BOND, BLOCKS, HID])).then_inc(wc_in, 16)
            for g in range(BLOCKS // NG):
                sp.wait_ge(n["v"], g + 1)
                sp.dma_start(v_rows[NG * g * NB:NG * (g + 1) * NB].rearrange("(k n) d -> n k d", n=NB),
                             vg[0:NB, g % 2, 0:NG]).then_inc(v_out[g % 2], 16)

            sp.wait_ge(phase["node"], 3)
            with sp.Fori(0, SLOT_STEPS // 2) as i:
                for u in range(2):
                    sp.wait_ge(rc_used, i * 2 + u + 1)
                    sp.dma_start(rec[:, u], slot_steps[bass.ds(i * 2 + u, 1)].rearrange(
                        "a p (t c) -> (a p) t c", c=REC)).then_inc(rc_in[u], 16)

            sp.wait_ge(f["out"], 1)
            full = NODES // NB
            sp.dma_start(out[0:full * NB].rearrange("(b n) d -> n b d", n=NB), x_blk[0:NB, 0:full]).then_inc(
                h_stored, 16)
            sp.dma_start(out[full * NB:NODES], x_blk[0:NODES - full * NB, full]).then_inc(h_stored, 16)
            sp.wait_ge(h_stored, 16 * (NT // 7 + 2))

        @block.gpsimd
        def _(pool):
            pool.iota(iota_b[:], [[1, BLOCKS]], base=0, channel_multiplier=0,
                      allow_small_or_imprecise_dtypes=True).then_inc(s_pool_const, 1)
            pool.iota(iota_n[:], [[1, NB]], base=1, channel_multiplier=0,
                      allow_small_or_imprecise_dtypes=True).then_inc(s_pool_const, 1)
            pool.iota(tile_no[:], [[1, TC]], base=0, channel_multiplier=TC,
                      allow_small_or_imprecise_dtypes=True).then_inc(s_pool_const, 1)
            pool.iota(lane[:], [[1, 1]], base=0, channel_multiplier=1,
                      allow_small_or_imprecise_dtypes=True).then_inc(s_pool_const, 1)
            pool.wait_ge(s_const, 9)
            pool.affine_select(out=before[:], in_=before[:], compare_op=ALU.is_gt, fill=0.0, base=0,
                               pattern=[[1, P]], channel_multiplier=-1).then_inc(s_pool_const, 1)
            pool.affine_select(out=not_before[:], in_=not_before[:], compare_op=ALU.is_ge, fill=0.0, base=0,
                               pattern=[[-1, P]], channel_multiplier=1).then_inc(s_pool_const, 1)
            pool.affine_select(out=ident[:], in_=ident[:], compare_op=ALU.not_equal, fill=1.0, base=0,
                               pattern=[[-1, P]], channel_multiplier=1).then_inc(s_pool_const, 1)

            pool.wait_ge(s_ld["xb"], 16)
            pool.wait_ge(s_ld["w"], 16 * WEIGHTS)
            pool.tensor_tensor(x_blk[0:NB], x_blk[0:NB], bo2_s[0:NB].unsqueeze(1).to_broadcast([NB, BLOCKS, HID]),
                               ALU.add).then_inc(xb_ready, 1)
            pool.wait_ge(tail_clear, 16 * (SLOT_STEPS - STEPS))
            pool.wait_ge(fill_ready, 1)
            pool.sem_inc(held)
            for b in range(BLOCKS):
                pool.indirect_dma_start(slots, bass.IndirectOffsetOnAxis(fill_i[:, b:b + 1], 0), zeros[:, 0:REC],
                                        None).then_inc(rec_out[b % 2], 16)
            for u in range(2):
                pool.wait_ge(rec_out[u], 16 * BLOCKS // 2)
            pool.wait_ge(h_stored, 16 * (NT // 7))
            pool.wait_ge(rel_stored, 48)
            pool.memset(sum1[:], 0.0).then_inc(sum1_clear, 1)

            def sort_moves(local):
                def gather(k, u):
                    pool.wait_ge(dst_ready, k + 1)
                    pool.sem_inc(held)
                    for t in range(STEP):
                        pool.indirect_dma_start(hj[:, u, t], None, h_rows,
                                                bass.IndirectOffsetOnAxis(dst_r[:, u, t:t + 1], 0)).then_inc(
                            hj_in[u], 16)

                def step(k, r, u, more):
                    if more and not local:
                        gather(k + 1, 1 - u)
                    pool.wait_ge(slot_ready, k + 1)
                    pool.wait_ge(rec_act, k + 1)
                    pool.wait_ge(rec_dve, k + 1)
                    pool.sem_inc(held)
                    for t in range(STEP):
                        pool.indirect_dma_start(slots, bass.IndirectOffsetOnAxis(slot_i[:, u, t:t + 1], 0),
                                                rec[:, u, t], None).then_inc(rec_out[u], 16)

                pairs(pool, STEPS, lambda: None if local else gather(0, 0), step)

            sort_path(pool, sort_moves)
            for u in range(2):
                pool.wait_ge(rec_out[u], 16 * (BLOCKS // 2 + TILES // 2))
            end(pool, "sort")

            for u in range(2):
                pool.wait_ge(v_out[u], 16 * (BLOCKS // NG // 2))
            with pool.Fori(0, SLOT_STEPS // 2) as i:
                for u in range(2):
                    pool.wait_ge(rc_in[u], i * 16 + 16)
                    pool.wait_ge(e["vg_used"], i * 2 + u + 1)
                    pool.sem_inc(held)
                    for t in range(STEP):
                        pool.indirect_dma_start(vg[:, u, t], None, v_rows,
                                                bass.IndirectOffsetOnAxis(rec_meta[:, u, t, 1:2], 0)).then_inc(
                            vg_in[u][t // 4], 16)

        @block.scalar
        def _(act):
            act.sem_inc(bond_used, 2)
            act.preload_act_table_set("natural_log_exp_and_others")
            def logs(k, u):
                act.wait_ge(zc_ready, k + 1)
                act.activation(e_s[:, u], z_s[:, u], ACT.Exp).then_inc(ex_ready, 1)
                act.wait_ge(ex_ready, k + 1)
                act.activation(e_s[:, u], e_s[:, u], ACT.Ln, bias=half[:, 0:1], scale=0.5).then_inc(ln_ready, 1)

            def step(k, r, u, more):
                if more:
                    logs(k + 1, 1 - u)
                act.wait_ge(bond_in[u], r * 16 + 16)
                act.wait_ge(rec_out[u], r * P + 16 * (BLOCKS // 2))
                act.activation(rec[:, u, :, R_BOND:R_BOND + BOND],
                               bond_s[:, u].rearrange("p (t c) -> p t c", c=BOND), ACT.Copy).then_inc(rec_act, 1)
                act.wait_ge(rec_act, k + 1)
                act.sem_inc(bond_used, 1)

            pairs(act, STEPS, lambda: logs(0, 0), step)
            end(act, "sort")

            G = BLOCKS // NG
            for g in range(G + 1):
                if g < G:
                    act.wait_ge(n["T"], g + 1)
                    act.activation(turned[:, g % 2, 0:2 * NB], ps[:, g % 2, 0:2 * NB], ACT.Copy).then_inc(n["Tc"], 1)
                    act.wait_ge(n["zc"], g + 1)
                    act.activation(e_s[:, g % 2, 0:NG * NB], z_s[:, g % 2, 0:NG * NB], ACT.Exp).then_inc(n["e"], 1)
                    act.wait_ge(n["e"], g + 1)
                    act.activation(e_s[:, g % 2, 0:NG * NB], e_s[:, g % 2, 0:NG * NB], ACT.Ln, bias=half[:, 0:1],
                                   scale=0.5).then_inc(n["l"], 1)
                if g >= 1:
                    act.wait_ge(n["xc"], g)
                    act.activation(act_s[0:NB, (g - 1) % 2], x_blk[0:NB, NG * (g - 1):NG * g],
                                   ACT.Square).then_inc(n["sq"], 1)
            act.wait_ge(n["var"], 1)
            act.activation(stat[0:NB, 2], stat[0:NB, 1], ACT.Sqrt).then_inc(n["std"], 1)
            for g in range(G):
                act.wait_ge(n["T2"], g + 1)
                act.activation(turned[:, g % 2], ps[:, 4 + g % 2, 0:NG * NB], ACT.Copy).then_inc(n["T2c"], 1)
                act.wait_ge(n["uv"], g + 1)
                if g >= 2:
                    act.wait_ge(v_out[g % 2], 16 * (g // 2))
                act.activation(vg[0:NB, g % 2, 0:NG], ps[0:NB, g % 2 * 2 + 1].rearrange("p (b d) -> p b d", d=HID),
                               ACT.Copy).then_inc(n["v"], 1)
            end(act, "node")

            act.wait_ge(phase["node"], 3)
            for u in range(2):
                act.wait_ge(v_out[u], 16 * (BLOCKS // NG // 2))
            act.preload_act_table(ACT.Silu)

            def turn(k, r, u):
                act.wait_ge(rc_in[u], r * 16 + 16)
                act.wait_ge(e["oh_used"], k + 1)
                act.activation(oh_n[:, u, :, NB:P], rec[:, u, :, R_BOND:R_BOND + BOND], ACT.Copy).then_inc(
                    e["bond"], 1)
                for q in range(2):
                    act.wait_ge(e["T"], k * 2 + (q + 1))
                    act.activation(oh_t[:, q], ps[:, q], ACT.Copy).then_inc(e["Tc"], 1)

            def step(k, r, u, more):
                for q in range(2):
                    act.wait_ge(e["add"], k * 2 + (q + 1))
                    act.activation(act_s[:, q], vg[:, u, 4 * q:4 * q + 4], ACT.Silu).then_inc(e["silu"], 1)
                act.wait_ge(e["silu"], k * 2 + 2)
                act.sem_inc(e["vg_used"], 1)
                if more:
                    turn(k + 1, *after(r, u))

            pairs(act, SLOT_STEPS, lambda: turn(0, 0, 0), step)
            end(act, "edge")

            for g in range(G):
                act.wait_ge(f["T"], g + 1)
                act.activation(turned[:, g % 2], ps[:, g % 2, 0:NG * NB], ACT.Copy).then_inc(f["Tc"], 1)
                act.wait_ge(f["xc"], g + 1)
                act.activation(act_s[0:NB, g % 2], x_blk[0:NB, NG * g:NG * (g + 1)], ACT.Square).then_inc(f["sq"], 1)
            act.wait_ge(f["var"], 1)
            act.activation(stat[0:NB, 2], stat[0:NB, 1], ACT.Sqrt).then_inc(f["std"], 1)

        @block.tensor
        def _(pe):
            pe.sem_inc(ft_used, 2)
            pe.sem_inc(oh_used, 2)
            pe.sem_inc(rb_used, 3)
            pe.wait_ge(s_ld["w"], 16 * WEIGHTS)
            pe.wait_ge(s_ld["xT"], 16)
            for g in range(NT // 7):
                if g >= 2:
                    pe.wait_ge(h_sbuf, g - 1)
                for t in range(7):
                    nodes = slice((7 * g + t) * P, (7 * g + t + 1) * P)
                    mm = pe.matmul(ps[:, g % 2, t * FILT:(t + 1) * FILT], xT_s[:, nodes], w_in_s[:],
                                   start=True, stop=True)
                mm.then_inc(h_psum, 1)

            pe.wait_ge(s_const, 9)
            pe.wait_ge(s_pool_const, 7)
            counts = ps[:, 2, 0:STEP * BLOCKS]
            pe.matmul(counts, zeros[:, 0:P], zeros[:, 0:STEP * BLOCKS], start=True, stop=True)
            with pe.Fori(0, STEPS // 2) as i:
                for u in range(2):
                    pe.wait_ge(oh_ready, i * 2 + u + 1)
                    pe.matmul(counts, ones_bf[:], oh_b[:, u].rearrange("p t b -> p (t b)"), start=False, stop=True,
                              skip_group_check=True).then_inc(oh_used, 1)
            pe.wait_ge(oh_used, 2 + STEPS)
            pe.sem_inc(cnt_ready, 1)

            run = ps[:, 4, 0:STEP * BLOCKS]
            pe.wait_ge(bases, 1)
            pe.matmul(run, ident[:], base[:].rearrange("p t b -> p (t b)"), start=True, stop=True)

            def sort_products(local):
                def filt(k, r, u):
                    pe.wait_ge(ft_in[u], r * 16 + 16)
                    pe.matmul(ps[0:FILT, u], wf1_s[:], fT_s[:, u, 0:SE // 2], start=True, stop=True)
                    pe.matmul(ps[FILT:P, u], wf1_s[:], fT_s[:, u, SE // 2:SE], start=True, stop=True).then_inc(
                        z_ready, 1)
                    pe.wait_ge(z_ready, k + 1)
                    pe.sem_inc(ft_used, 1)

                def rank(k, u):
                    pe.wait_ge(oh_ready, k + (STEPS + 1))
                    pe.matmul(run, before[:], oh_b[:, u].rearrange("p t b -> p (t b)"), start=False, stop=True,
                              skip_group_check=True).then_inc(rank_ready, 1)

                def whole(k, u):
                    pe.wait_ge(rank_read, k + 1)
                    pe.matmul(run, not_before[:], oh_b[:, u].rearrange("p t b -> p (t b)"), start=False, stop=True,
                              skip_group_check=True).then_inc(oh_used, 1)

                def first():
                    if local:
                        pe.sem_inc(hj_psum, 2)
                    filt(0, 0, 0)
                    filt(1, 0, 1)
                    rank(0, 0)
                    whole(0, 0)

                def step(k, r, u, more, filt_too=True):
                    if local:
                        pe.wait_ge(win_in[u], r * 32 + 32)
                        pe.wait_ge(on_dst_ready, k + 3)
                        for j in range(4):
                            mm = pe.matmul(ps[:, 5 + u, j * P:(j + 1) * P], on_dst[:, u, j * P:(j + 1) * P],
                                           h_win[:, u], start=True, stop=True)
                        mm.then_inc(hj_psum, 1)
                    pe.wait_ge(sp_ready, k + 1)
                    pe.matmul(ps[:, 2 + u], one_row[:], bf2_s[:], start=True, stop=True)
                    for j in range(4):
                        mm = pe.matmul(ps[:, 2 + u, j * P:(j + 1) * P], sp_s[:, u, j * P:(j + 1) * P], wf2_s[:],
                                       start=False, stop=True, skip_group_check=True)
                    mm.then_inc(wt_ready, 1)
                    if more:
                        rank(k + 1, 1 - u)
                        if filt_too:
                            filt(k + 2, r + 1, u)
                        whole(k + 1, 1 - u)

                first()
                with pe.Fori(0, STEPS // 2 - 1) as i:
                    for u in range(2):
                        step(i * 2 + u, i, u, True)
                step(STEPS - 2, STEPS // 2 - 1, 0, True, filt_too=False)
                step(STEPS - 1, STEPS // 2 - 1, 1, False)

            sort_path(pe, sort_products)
            end(pe, "sort")

            pe.wait_ge(s_ld["table"], 16)
            pe.wait_ge(phase["sort"], 4)
            for k in range(BANKS):
                pe.matmul(ps[:, k], zeros[:, 0:P], zeros[:, 0:512], start=True, stop=True)
            flat = ps[:].rearrange("p k n -> p (k n)")
            with pe.Fori(0, SLOT_STEPS // 3) as i:
                for u in range(3):
                    _, at = nc.values_load_multi_w_load_instructions(
                        table[1:2, bass.ds(i * (3 * STEP) + u * STEP, STEP)], PE_ONLY, min_val=0,
                        max_val=(BANKS - 1) * 512 + (PER_BANK - 1) * MSG,
                        skip_runtime_bounds_check_because="clamped to the last block when the table is made")
                    pe.wait_ge(rb_in[u], i * 16 + 16)
                    pe.wait_ge(ohn_ready, i * 3 + u + 1)
                    for t in range(STEP):
                        mm = pe.matmul(flat[0:NB, bass.ds(at[t], WIDE)], sum_oh[u][:, t, 0:NB],
                                       sum_rec[u][:, t, 0:WIDE], start=False, stop=True, skip_group_check=True)
                    mm.then_inc(rb_used, 1)
            pe.wait_ge(rb_used, 3 + SLOT_STEPS)
            pe.sem_inc(sum_done, 1)

            pe.wait_ge(sum0_ready, 1)
            G = BLOCKS // NG
            for g in range(G + 1):
                if g < G:
                    if g >= 2:
                        pe.wait_ge(n["Tc"], g - 1)
                    for q in range(2):
                        b = NG * g + 2 * q
                        mm = pe.transpose(ps[:, g % 2, q * NB:(q + 1) * NB],
                                          sum0[0:NB, b:b + 2].rearrange("p b f -> p (b f)"), ident[0:NB, 0:NB])
                    mm.then_inc(n["T"], 1)
                    pe.wait_ge(n["Tc"], g + 1)
                    for j in range(NG):
                        half_ = slice(FILT * (j % 2), FILT * (j % 2) + FILT)
                        mm = pe.matmul(ps[:, 2 + 4 * (g % 2) + j % 2, j // 2 * NB:(j // 2 + 1) * NB], wo1_s[half_, :],
                                       turned[half_, g % 2, j // 2 * NB:(j // 2 + 1) * NB], start=True, stop=True)
                    mm.then_inc(n["z"], 1)
                if g >= 1:
                    p = g - 1
                    pe.wait_ge(n["sp"], g)
                    if g >= 3:
                        pe.wait_ge(n["xc"], g - 2)
                    for j in range(NG):
                        at_ = j % 2 * (NG // 2) + j // 2
                        mm = pe.matmul(ps[0:NB, 4 + p % 2, j * HID:(j + 1) * HID],
                                       sp_s[:, p % 2, at_ * NB:(at_ + 1) * NB], wo2_s[:], start=True, stop=True)
                    mm.then_inc(n["o"], 1)
            for g in range(G):
                pe.wait_ge(n["x1"], g + 1)
                for j in range(NG):
                    mm = pe.transpose(ps[:, 4 + g % 2, j * NB:(j + 1) * NB], x_blk[0:NB, NG * g + j],
                                      ident[0:NB, 0:NB])
                mm.then_inc(n["T2"], 1)
                pe.wait_ge(n["T2c"], g + 1)
                if g >= 2:
                    pe.wait_ge(n["u"], g - 1)
                    pe.wait_ge(n["v"], g - 1)
                for j in range(NG):
                    for k in range(2):
                        mm = pe.matmul(ps[0:NB, g % 2 * 2 + k, j * HID:(j + 1) * HID],
                                       turned[:, g % 2, j * NB:(j + 1) * NB], wab_s[:, k * HID:(k + 1) * HID],
                                       start=True, stop=True)
                mm.then_inc(n["uv"], 1)
            end(pe, "node")

            pe.wait_ge(phase["node"], 3)
            pe.wait_ge(wc_in, 16)
            src_flat = src_w[:].rearrange("p b d -> p (b d)")

            def block_rows(k):
                _, at = nc.values_load_multi_w_load_instructions(
                    table[0:1, bass.ds(k * STEP, STEP)], PE_ONLY, min_val=0, max_val=(BLOCKS - 1) * HID,
                    skip_runtime_bounds_check_because="clamped to the last block when the table is made")
                return at

            def spread(k, u, at):
                pe.wait_ge(e["oh"], k + 1)
                pe.wait_ge(e["bond"], k + 1)
                for q in range(2):
                    for t in range(4):
                        mm = pe.transpose(ps[:, q, t * P:(t + 1) * P], oh_n[:, u, 4 * q + t], ident[:])
                    mm.then_inc(e["T"], 1)
                for q in range(2):
                    pe.wait_ge(e["Tc"], k * 2 + (q + 1))
                    for t in range(4):
                        mm = pe.matmul(ps[:, 2 + 2 * u + q, t * HID:(t + 1) * HID], oh_t[:, q, t * P:(t + 1) * P],
                                       src_flat[:, bass.ds(at[4 * q + t], HID)], start=True, stop=True)
                    mm.then_inc(e["pre"], 1)

            def step(k, r, u, more):
                if more:
                    at = block_rows(k + 1)
                for q in range(2):
                    pe.wait_ge(e["silu"], k * 2 + (q + 1))
                    pe.wait_ge(e["acc"], k * 8 + 4 * (q + 1))
                    for t in range(4):
                        mm = pe.matmul(ps[0:NB, 6 + q, t * HID:(t + 1) * HID], oh_n[:, u, 4 * q + t, 0:NB],
                                       act_s[:, q, t], start=True, stop=True)
                    mm.then_inc(e["agg"], 1)
                pe.wait_ge(e["agg"], k * 2 + 2)
                pe.sem_inc(e["oh_used"], 1)
                if more:
                    spread(k + 1, 1 - u, at)

            pairs(pe, SLOT_STEPS, lambda: spread(0, 0, block_rows(0)), step)
            end(pe, "edge")

            pe.wait_ge(phase["edge"], 3)
            for g in range(G):
                if g >= 2:
                    pe.wait_ge(f["Tc"], g - 1)
                for j in range(NG):
                    mm = pe.transpose(ps[:, g % 2, j * NB:(j + 1) * NB], sum1[0:NB, NG * g + j], ident[0:NB, 0:NB])
                mm.then_inc(f["T"], 1)
                pe.wait_ge(f["Tc"], g + 1)
                if g >= 2:
                    pe.wait_ge(f["xc"], g - 1)
                for j in range(NG):
                    mm = pe.matmul(ps[0:NB, 2 + g % 2, j * HID:(j + 1) * HID], turned[:, g % 2, j * NB:(j + 1) * NB],
                                   w2_s[:], start=True, stop=True)
                mm.then_inc(f["y"], 1)

        @block.vector
        def _(dve):
            for to, v in ((zeros, 0.0), (wf2_s, 0.0), (h_win, 0.0), (ones_bf, 1.0), (before, 1.0), (not_before, 1.0),
                          (ident, 0.0), (half, 0.5), (one_row, 1.0), (rec, 0.0)):
                dve.memset(to[:], v).then_inc(s_const, 1)
            dve.wait_ge(s_const, 10)
            dve.memset(rec[:, :, :, R_ONE:R_ONE + 1], 1.0).then_inc(s_const, 1)

            dve.wait_ge(s_ld["edges"], 48)
            dve.tensor_scalar(blk_i, src_i, 1.0 / NB, 0.5 / NB - 0.5, ALU.mult, ALU.add).then_inc(prep, 1)
            dve.tensor_scalar(src_1, src_i, 1.0, None, ALU.add).then_inc(prep, 1)
            dve.tensor_copy(meta[:, :, 1], dst_i).then_inc(prep, 1)
            dve.wait_ge(prep, 1)
            dve.tensor_copy(blk_f[:], blk_i).then_inc(prep, 1)
            dve.wait_ge(prep, 4)
            dve.scalar_tensor_tensor(out=meta[:, :, 0], in0=blk_f[:], scalar=-float(NB), in1=src_1, op0=ALU.mult,
                                     op1=ALU.add).then_inc(prep, 1)
            dve.wait_ge(s_ld["w"], 16 * WEIGHTS)
            dve.tensor_scalar(bf1_l[:], bf1_s[:], -LOG2, None, ALU.add).then_inc(prep, 1)
            dve.tensor_scalar(bo1_l[:], bo1_s[:], -LOG2, None, ALU.add).then_inc(prep, 1)

            for g in range(NT // 7):
                dve.wait_ge(h_psum, g + 1)
                dve.tensor_tensor(h_s[:, 7 * g:7 * g + 7], ps[:, g % 2, 0:7 * FILT].rearrange("p (t f) -> p t f", f=FILT),
                                  b_in_s[:].unsqueeze(1).to_broadcast([P, 7, FILT]), ALU.add).then_inc(h_sbuf, 1)

            def one_hot_block(k, u):
                return dve.tensor_tensor(oh_b[:, u], blk_f[:, bass.ds(k * STEP, STEP)].unsqueeze(2).to_broadcast(
                    [P, STEP, BLOCKS]), iota_b[:].unsqueeze(1).to_broadcast([P, STEP, BLOCKS]), ALU.is_equal)

            dve.wait_ge(s_pool_const, 7)
            dve.wait_ge(prep, 7)
            with dve.Fori(0, STEPS // 2) as i:
                for u in range(2):
                    dve.wait_ge(oh_used, i * 2 + u + 1)
                    one_hot_block(i * 2 + u, u).then_inc(oh_ready, 1)

            dve.wait_ge(s_ld["dst_2"], 16)
            dve.tensor_reduce(win_f[:, 0], dst_2, X, ALU.min).then_inc(win_part, 1)
            dve.tensor_reduce(win_f[:, 1], dst_2, X, ALU.max).then_inc(win_part, 1)
            dve.wait_ge(win_part, 2)
            dve.tensor_scalar(win_f[:, 2], win_f[:, 0], float(NPAD - WIN), None, ALU.min).then_inc(win_part, 1)
            dve.wait_ge(win_part, 3)
            dve.tensor_copy(win_i[:, 0], win_f[:, 2])
            dve.tensor_tensor(win_i[:, 1], win_f[:, 1], win_f[:, 2], ALU.subtract)
            for k in range(2):
                last = dve.tensor_scalar(rel_2[:, k], dst_2[:, k], win_f[:, 2, k:k + 1], None, ALU.subtract)
            last.then_inc(win_ready, 1)
            dve.tensor_scalar(lane_half[0:WIN], lane[0:WIN], 0.0, None, ALU.add)
            dve.tensor_scalar(lane_half[WIN:P], lane[WIN:P], -float(WIN), None, ALU.add).then_inc(win_part, 1)

            dve_n = [0]

            def link(ins, s=n["dve"]):
                dve_n[0] += 1
                ins.then_inc(s, 1)
                dve.wait_ge(s, dve_n[0])

            total, ntile, end_t, start_t, one, last_t, pos_b = (blkn[:, j] for j in range(7))
            dve.wait_ge(cnt_ready, 1)
            link(dve.tensor_copy(cnt[:], ps[:, 2, 0:STEP * BLOCKS].rearrange("p (t b) -> p t b", b=BLOCKS)))
            link(dve.tensor_reduce(total, cnt[:].rearrange("p t b -> p b t"), X, ALU.add))
            link(dve.tensor_scalar(ntile_i[:], total, 1.0 / P, (P - 1) / 2.0 / P, ALU.mult, ALU.add))
            link(dve.memset(one, 1.0))
            link(dve.tensor_copy(ntile, ntile_i[:]))
            link(dve.tensor_tensor_scan(end_t, one, ntile, 0.0, ALU.mult, ALU.add))
            link(dve.tensor_tensor(start_t, end_t, ntile, ALU.subtract))
            link(dve.tensor_scalar(base[:, 0], start_t, float(P), None, ALU.mult))
            for t in range(1, STEP):
                link(dve.tensor_tensor(base[:, t], base[:, t - 1], cnt[:, t - 1], ALU.add))
            dve.sem_inc(bases, 1)
            link(dve.tensor_scalar(last_t, end_t, -1.0, 0.0, ALU.add, ALU.max))
            link(dve.tensor_scalar(pos_b, last_t, float(P), lane[:, 0:1], ALU.mult, ALU.add))
            link(dve.tensor_copy(pos_i[:], pos_b))
            link(slot_rows(dve, prep, 7, pos_i[:], [bits[:, j] for j in range(3)], fill_i[:]))
            dve.sem_inc(fill_ready, 1)
            link(dve.tensor_tensor(cmp, tile_no[:].unsqueeze(2).to_broadcast([P, TC, BLOCKS]),
                                   end_t.unsqueeze(1).to_broadcast([P, TC, BLOCKS]), ALU.is_ge))
            link(dve.tensor_reduce(tabf[:, 0], cmp, X, ALU.add))
            link(dve.tensor_scalar(tabf[:, 0], tabf[:, 0], float(BLOCKS - 1), None, ALU.min))
            link(dve.tensor_scalar(tabi[:, 2], tabf[:, 0], 1.0 / PER_BANK, 0.5 / PER_BANK - 0.5, ALU.mult, ALU.add))
            link(dve.tensor_copy(tabf[:, 1], tabi[:, 2]))
            link(dve.tensor_scalar(tabf[:, 2], tabf[:, 0], float(MSG), None, ALU.mult))
            link(dve.tensor_scalar(tabi[:, 0], tabf[:, 0], float(HID), None, ALU.mult))
            link(dve.scalar_tensor_tensor(out=tabi[:, 1], in0=tabf[:, 1], scalar=float(512 - PER_BANK * MSG),
                                          in1=tabf[:, 2], op0=ALU.mult, op1=ALU.add))
            dve.sem_inc(tab_ready, 1)

            dve.wait_ge(s_ld["win"], 16)
            link(dve.tensor_reduce(reach[:], win_s[:, 1], X, ALU.max))
            link(dve.tensor_scalar(is_local[:], reach[:], float(WIN - 1), None, ALU.is_le))
            dve.sem_inc(path_ready, 1)
            dve.wait_ge(win_part, 4)

            SLOT_LINKS, REC_LINKS = 7, 3

            def sort_vectors(local):
                def first_half(k, r, u):
                    dve.wait_ge(oh_used, k + (STEPS + 1))
                    one_hot_block(k, u).then_inc(oh_ready, 1)
                    dve.wait_ge(z_ready, k + 1)
                    dve.tensor_scalar(z_s[:, u], ps[:, u], bf1_s[:, 0:1], CAP, ALU.add, ALU.min).then_inc(zc_ready, 1)
                    if local:
                        dve.wait_ge(rel_in[u], r * 32 + 32)
                        dve.wait_ge(hj_psum, k + 1)
                        dve.tensor_scalar(on_dst[:, u], rel_s[:, u], lane_half[:, 0:1], None,
                                          ALU.is_equal).then_inc(on_dst_ready, 1)
                    else:
                        dve.tensor_copy(dst_r[:, u], meta[:, bass.ds(k * STEP, STEP), 1]).then_inc(dst_ready, 1)

                def rank(k, u):
                    dve.wait_ge(rank_ready, k + 1)
                    dve.tensor_tensor(rank_m[:], ps[:, 4, 0:STEP * BLOCKS].rearrange("p (t b) -> p t b", b=BLOCKS),
                                      oh_b[:, u], ALU.mult).then_inc(rank_read, 1)

                def slot(k, u):
                    done = k * SLOT_LINKS
                    dve.wait_ge(rank_read, k + 1)
                    dve.tensor_reduce(pos_f[:, 0:STEP], rank_m[:], X, ALU.add).then_inc(dve_slot, 1)
                    dve.wait_ge(dve_slot, done + 1)
                    dve.tensor_copy(pos_i[:, 0:STEP], pos_f[:, 0:STEP]).then_inc(dve_slot, 1)
                    dve.wait_ge(dve_slot, done + 2)
                    slot_rows(dve, dve_slot, done + 2, pos_i[:, 0:STEP], [bits[:, j, 0:STEP] for j in range(3)],
                              slot_n[:, u]).then_inc(dve_slot, 1)

                def softplus(k, u):
                    dve.wait_ge(ln_ready, k + 1)
                    dve.scalar_tensor_tensor(out=sp_s[:, u], in0=ps[:, u], scalar=bf1_l[:, 0:1], in1=e_s[:, u],
                                             op0=ALU.add, op1=ALU.max).then_inc(sp_ready, 1)

                def first():
                    if local:
                        dve.sem_inc(on_dst_ready, 2)
                    first_half(0, 0, 0)
                    rank(0, 0)
                    slot(0, 0)
                    softplus(0, 0)

                def step(k, r, u, more):
                    if more:
                        first_half(k + 1, *after(r, u))
                    halves = lambda v: v.rearrange("p (j a f) -> p a j f", a=2, f=FILT)
                    dve.wait_ge(wt_ready, k + 1)
                    dve.tensor_tensor(wt[:].rearrange("p (a j) f -> p a j f", a=2), halves(ps[:, 2 + u]),
                                      w_s[:, bass.ds(k * STEP, STEP)].rearrange("p (a j) -> p a j", a=2).unsqueeze(
                                          3).to_broadcast([P, 2, 4, FILT]), ALU.mult).then_inc(dve_rec, 1)
                    if more:
                        rank(k + 1, 1 - u)
                    dve.wait_ge(rec_out[u], r * P + 16 * (BLOCKS // 2))
                    dve.wait_ge(dve_slot, k * SLOT_LINKS + SLOT_LINKS)
                    dve.tensor_copy(slot_i[:, u], slot_n[:, u]).then_inc(slot_ready, 1)
                    dve.tensor_copy(rec_meta[:, u], meta[:, bass.ds(k * STEP, STEP), :]).then_inc(dve_rec, 1)
                    dve.wait_ge(dve_rec, k * REC_LINKS + 1)
                    if local:
                        dve.wait_ge(hj_psum, k + 3)
                        dve.tensor_tensor(rec[:, u, :, 0:FILT].rearrange("p (a j) f -> p a j f", a=2),
                                          wt[:].rearrange("p (a j) f -> p a j f", a=2), halves(ps[:, 5 + u]),
                                          ALU.mult).then_inc(dve_rec, 1)
                    else:
                        dve.wait_ge(hj_in[u], r * P + P)
                        dve.tensor_tensor(rec[:, u, :, 0:FILT], wt[:], hj[:, u], ALU.mult).then_inc(dve_rec, 1)
                    if more:
                        slot(k + 1, 1 - u)
                    dve.wait_ge(dve_rec, k * REC_LINKS + REC_LINKS)
                    dve.sem_inc(rec_dve, 1)
                    if more:
                        softplus(k + 1, 1 - u)

                pairs(dve, STEPS, first, step)

            sort_path(dve, sort_vectors)
            end(dve, "sort")

            def one_hot_node(to, of):
                place = of.bitcast(I32)[:, :, R_META:R_META + 1]
                return dve.tensor_tensor(to[:, :, 0:NB], place.to_broadcast([P, STEP, NB]),
                                         iota_n[:].unsqueeze(1).to_broadcast([P, STEP, NB]), ALU.is_equal)

            with dve.Fori(0, SLOT_STEPS // 3) as i:
                for u in range(3):
                    dve.wait_ge(rb_in[u], i * 16 + 16)
                    dve.wait_ge(rb_used, i * 3 + u + 1)
                    one_hot_node(sum_oh[u], sum_rec[u]).then_inc(ohn_ready, 1)
            dve.wait_ge(sum_done, 1)
            for k in range(BANKS):
                sums = ps[0:NB, k, 0:PER_BANK * MSG].rearrange("p (b f) -> p b f", f=MSG)
                dve.tensor_copy(sum0[0:NB, PER_BANK * k:PER_BANK * (k + 1)], sums[:, :, 0:FILT])
                last = dve.tensor_copy(deg[0:NB, PER_BANK * k:PER_BANK * (k + 1)], sums[:, :, FILT])
            last.then_inc(sum0_ready, 1)
            end(dve, "sum")

            G = BLOCKS // NG
            dve.wait_ge(xb_ready, 1)

            def centre(g, s, into):
                blocks = slice(NG * g, NG * (g + 1))
                link(dve.tensor_reduce(stat[0:NB, 0, blocks], x_blk[0:NB, blocks], X, ALU.add), s)
                link(dve.tensor_scalar(stat[0:NB, 0, blocks], stat[0:NB, 0, blocks], -1.0 / HID, None, ALU.mult), s)
                dve.tensor_tensor(x_blk[0:NB, blocks], x_blk[0:NB, blocks],
                                  stat[0:NB, 0, blocks].unsqueeze(2).to_broadcast([NB, NG, HID]),
                                  ALU.add).then_inc(into, 1)

            def square_sum(g, sq):
                dve.wait_ge(sq, g + 1)
                return dve.tensor_reduce(stat[0:NB, 1, NG * g:NG * (g + 1)], act_s[0:NB, g % 2], X, ALU.add)

            for g in range(G + 1):
                if g < G:
                    dve.wait_ge(n["z"], g + 1)
                    z = ps[:, 2 + 4 * (g % 2):4 + 4 * (g % 2), 0:2 * NB]
                    both = lambda v: v[:, g % 2, 0:NG * NB].rearrange("p (a n) -> p a n", a=2)
                    dve.tensor_scalar(both(z_s), z, bo1_s[:, 0:1], CAP, ALU.add, ALU.min).then_inc(n["zc"], 1)
                    dve.wait_ge(n["l"], g + 1)
                    dve.scalar_tensor_tensor(out=both(sp_s), in0=z, scalar=bo1_l[:, 0:1], in1=both(e_s), op0=ALU.add,
                                             op1=ALU.max).then_inc(n["sp"], 1)
                if g >= 1:
                    p = g - 1
                    dve.wait_ge(n["o"], g)
                    link(dve.tensor_tensor(x_blk[0:NB, NG * p:NG * g], x_blk[0:NB, NG * p:NG * g],
                                           ps[0:NB, 4 + p % 2].rearrange("p (b d) -> p b d", d=HID), ALU.add))
                    centre(p, n["dve"], n["xc"])
                    link(square_sum(p, n["sq"]))

            def deviation(s, var, std):
                dve.tensor_scalar(stat[0:NB, 1], stat[0:NB, 1], 1.0 / HID, EPS, ALU.mult, ALU.add).then_inc(var, 1)
                dve.wait_ge(std, 1)
                link(dve.reciprocal(stat[0:NB, 3], stat[0:NB, 2]), s)

            def scale(g):
                blocks = slice(NG * g, NG * (g + 1))
                return dve.tensor_tensor(x_blk[0:NB, blocks], x_blk[0:NB, blocks],
                                         stat[0:NB, 3, blocks].unsqueeze(2).to_broadcast([NB, NG, HID]), ALU.mult)

            deviation(n["dve"], n["var"], n["std"])
            for g in range(G + 1):
                if g < G:
                    scale(g).then_inc(n["x1"], 1)
                if g >= 1:
                    p = g - 1
                    dve.wait_ge(n["uv"], g)
                    dve.tensor_tensor(src_w[0:NB, NG * p:NG * g], ps[0:NB, p % 2 * 2].rearrange("p (b d) -> p b d", d=HID),
                                      b1_s[0:NB].unsqueeze(1).to_broadcast([NB, NG, HID]), ALU.add).then_inc(n["u"], 1)
            end(dve, "node")

            dve.wait_ge(phase["node"], 3)
            dve.wait_ge(sum1_clear, 1)
            dve.sem_inc(rc_used, 2)
            dve.sem_inc(e["oh_used"], 2)
            dve.sem_inc(e["vg_used"], 2)
            dve.sem_inc(e["acc"], 8)
            sum_flat = sum1[:].rearrange("p b d -> p (b d)")

            def one_hot(k, r, u):
                dve.wait_ge(rc_in[u], r * 16 + 16)
                dve.wait_ge(e["oh_used"], k + 1)
                one_hot_node(oh_n[:, u], rec[:, u]).then_inc(e["oh"], 1)

            def step(k, r, u, more):
                _, at = nc.values_load_multi_w_load_instructions(
                    table[0:1, bass.ds(k * STEP, STEP)], DVE_ONLY, min_val=0, max_val=(BLOCKS - 1) * HID,
                    skip_runtime_bounds_check_because="clamped to the last block when the table is made")
                for q in range(2):
                    dve.wait_ge(vg_in[u][q], r * 64 + 64)
                    dve.wait_ge(e["pre"], k * 2 + (q + 1))
                    rows = vg[:, u, 4 * q:4 * q + 4]
                    dve.tensor_tensor(rows, rows, ps[:, 2 + 2 * u + q].rearrange("p (t d) -> p t d", d=HID),
                                      ALU.add).then_inc(e["add"], 1)
                dve.wait_ge(e["bond"], k + 1)
                dve.sem_inc(rc_used, 1)
                if more:
                    one_hot(k + 1, *after(r, u))
                for q in range(2):
                    dve.wait_ge(e["agg"], k * 2 + (q + 1))
                    for t in range(4):
                        dve.wait_ge(e["acc"], k * 8 + (4 * q + t + 8))
                        here = sum_flat[0:NB, bass.ds(at[4 * q + t], HID)]
                        dve.tensor_tensor(here, here, ps[0:NB, 6 + q, t * HID:(t + 1) * HID], ALU.add).then_inc(
                            e["acc"], 1)

            pairs(dve, SLOT_STEPS, lambda: one_hot(0, 0, 0), step)
            end(dve, "edge")

            dve_n[0] = 0
            for g in range(G):
                dve.wait_ge(f["y"], g + 1)
                blocks = slice(NG * g, NG * (g + 1))
                link(dve.tensor_tensor(x_blk[0:NB, blocks], x_blk[0:NB, blocks],
                                       ps[0:NB, 2 + g % 2].rearrange("p (b d) -> p b d", d=HID), ALU.add), f["dve"])
                for b in range(NG * g, NG * (g + 1)):
                    ins = dve.scalar_tensor_tensor(out=x_blk[0:NB, b], in0=b2_s[0:NB], scalar=deg[0:NB, b:b + 1],
                                                   in1=x_blk[0:NB, b], op0=ALU.mult, op1=ALU.add)
                link(ins, f["dve"])
                centre(g, f["dve"], f["xc"])
                link(square_sum(g, f["sq"]), f["dve"])
            deviation(f["dve"], f["var"], f["std"])
            for g in range(G):
                ins = scale(g)
            ins.then_inc(f["out"], 1)


_OUT = ((NODES, HID), np.float32)


def kernel(**inputs):
    import concourse.bacc as bacc
    from concourse.bass_utils import run_bass_kernel_spmd

    a = {k: np.asarray(v) for k, v in inputs.items()}

    def edges(v, fill):
        rest = np.full((PADDED - EDGES,) + v.shape[1:], fill, v.dtype)
        return np.concatenate([v, rest])

    def by_tile(v, fill):
        return np.ascontiguousarray(edges(v, fill).reshape(TILES, P).T)

    x = np.concatenate([a["x"], np.zeros((NPAD - NODES, HID), np.float32)])
    laid = {
        "xT": np.ascontiguousarray(x.T),
        "xb": np.ascontiguousarray(x.reshape(BLOCKS, NB, HID).transpose(1, 0, 2)),
        "src": by_tile(a["src"], NODES),
        "dst": by_tile(a["dst"], 0),
        "dst_steps": edges(a["dst"], NODES - 1).reshape(STEPS, SE),
        "weight": by_tile(a["edge_weight"], 0),
        "fT": np.ascontiguousarray(edges(a["edge_attr_32"], 0).reshape(STEPS, SE, RBF).transpose(0, 2, 1)),
        "bond": np.ascontiguousarray(edges(a["edge_attr_16"], 0).reshape(STEPS, STEP, P, BOND).transpose(
            0, 2, 1, 3).reshape(STEPS, P, STEP * BOND)),
    }
    for name in ("w_in", "b_in", "w_f1", "b_f1", "w_f2", "b_f2", "w_o1", "b_o1", "w_o2", "b_o2"):
        laid[name] = np.ascontiguousarray(a["L0_gnn_" + name])
    for name in ("W1", "b1", "W2", "b2"):
        laid[name] = np.ascontiguousarray(a["L1_gnn_" + name])
    nc = bacc.Bacc("TRN2", target_bir_lowering=False, num_devices=1)
    args = {k: nc.dram_tensor("in_" + k, v.shape, mybir.dt.from_np(v.dtype), kind="ExternalInput").ap()
            for k, v in laid.items()}
    out = nc.dram_tensor("out", _OUT[0], F32, kind="ExternalOutput").ap()
    build(nc, out=out, **args)
    r = run_bass_kernel_spmd(nc, [{"in_" + k: v for k, v in laid.items()}], core_ids=[0])
    return r.results[0]["out"]
```

```python
from contextlib import ExitStack

import numpy as np

import concourse.bass as bass
from concourse import mybir

ALU = mybir.AluOpType
ACT = mybir.ActivationFunctionType
F32 = mybir.dt.float32
I32 = mybir.dt.int32
BF16 = mybir.dt.bfloat16
X = mybir.AxisListType.X
PE_ONLY = (mybir.EngineType.PE,)
DVE_ONLY = (mybir.EngineType.DVE,)

P = 128
NODES, HID, FILT, RBF, BOND = 6250, 128, 64, 32, 16
EDGES = 206250
NB = HID - BOND
BLOCKS = -(-NODES // NB)
STEP = 8
SE = STEP * P
TILES = -(-EDGES // (2 * SE)) * 2 * STEP
STEPS = TILES // STEP
PADDED = TILES * P
SLOT_TILES = -(-(TILES + BLOCKS) // STEP) * STEP
SLOT_STEPS = SLOT_TILES // STEP
SLOTS = SLOT_TILES * P
TC = -(-SLOT_TILES // P)
MSG = FILT + 1
WIDE = 96
REC = P
R_ONE, R_BOND, R_META = FILT, WIDE, WIDE + BOND
WIN = 64
NPAD = BLOCKS * NB
NT = NPAD // P
assert NPAD == NT * P and TILES * P == PADDED
PER_BANK = 512 // MSG
BANKS = 8
assert PER_BANK * BANKS >= BLOCKS and (PER_BANK - 1) * MSG + WIDE <= 512
PARTS = NT // 7
assert NT % 7 == 0 and BLOCKS % (4 * PARTS) == 0
CLEARS = 12
NG = 4
LOG2 = float(np.log(2.0))
CAP = 30.0
EPS = 1e-5


def build(nc, xT, xb, src, dst, dst_steps, weight, fT, bond, w_in, b_in, w_f1, b_f1, w_f2, b_f2, w_o1, b_o1, w_o2, b_o2,
          W1, b1, W2, b2, out):
    h_rows = nc.dram_tensor("h_rows", (NPAD, FILT), F32).ap()
    v_rows = nc.dram_tensor("v_rows", (NPAD, HID), F32).ap()
    slots = nc.dram_tensor("slots", (SLOTS, REC), F32).ap()
    rel_rows = nc.dram_tensor("rel_rows", (STEPS, SE), BF16).ap()
    win_table = nc.dram_tensor("win_table", (2, STEPS), I32).ap()
    tile_table = nc.dram_tensor("tile_table", (2, P * TC), I32).ap()
    slot_steps = slots.rearrange("(g p t) c -> g p (t c)", p=P, t=STEP)

    with ExitStack() as ctx:
        def sb(name, shape, dt=F32):
            return ctx.enter_context(nc.sbuf_tensor(name, shape, dt))

        def sem(name):
            return ctx.enter_context(nc.semaphore(name))

        def sems(name, n=2):
            return [sem(f"{name}{k}") for k in range(n)]

        ps = ctx.enter_context(nc.psum_tensor("ps", [P, BANKS, 512], F32))

        zeros = sb("zeros", [P, STEP * REC])
        ones = sb("ones", [P, P])
        ident = sb("ident", [P, P])
        ones_bf = sb("ones_bf", [P, P], BF16)
        before = sb("before", [P, P], BF16)
        not_before = sb("not_before", [P, P], BF16)
        iota_b = sb("iota_b", [P, BLOCKS])
        iota_n = sb("iota_n", [P, NB])
        tile_no = sb("tile_no", [P, TC])
        lane = sb("lane", [P, 1])
        half = sb("half", [P, 1])
        lane_i = sb("lane_i", [P, 1], I32)
        lane_8 = sb("lane_8", [P, STEP])
        tile_cnt = sb("tile_cnt", [P, BLOCKS])
        lane_half = sb("lane_half", [P, 1])
        w_in_s = sb("w_in_s", [P, FILT])
        b_in_s = sb("b_in_s", [P, FILT])
        wf1_s = sb("wf1_s", [2 * RBF, P])
        bf1_s = sb("bf1_s", [P, 1])
        bf1_l = sb("bf1_l", [P, 1])
        wf2_s = sb("wf2_s", [P, P])
        bf2_s = sb("bf2_s", [1, STEP * FILT])
        wo1_s = sb("wo1_s", [P, HID])
        bo1_s = sb("bo1_s", [P, 1])
        bo1_l = sb("bo1_l", [P, 1])
        wo2_s = sb("wo2_s", [P, HID])
        bo2_s = sb("bo2_s", [P, HID])
        wab_s = sb("wab_s", [P, 2 * HID])
        b1_s = sb("b1_s", [P, HID])
        w2_s = sb("w2_s", [P, HID])
        b2_s = sb("b2_s", [P, HID])

        x_blk = sb("x_blk", [P, BLOCKS, HID])
        src_w = sb("src_w", [P, BLOCKS, HID])
        xT_s = src_w[:, :, :].rearrange("p b d -> p (b d)")[:, 0:NPAD]
        sum1 = sb("sum1", [P, BLOCKS, HID])
        h_s = sum1[:, :, :].rearrange("p b d -> p (b d)")[:, 0:NT * FILT].rearrange("p (t f) -> p t f", f=FILT)
        sum0 = sb("sum0", [P, BLOCKS, FILT])
        deg = sb("deg", [P, BLOCKS])
        src_1 = sum0[:, :, :].rearrange("p b f -> p (b f)")[:, 0:TILES]
        src_i = sum0[:, :, :].rearrange("p b f -> p (b f)")[:, TILES:2 * TILES].bitcast(I32)
        w_s = sb("w_s", [P, TILES])
        blk_f = sb("blk_f", [P, TILES])
        meta = sb("meta", [P, TILES, 2], I32)
        table = sb("table", [2, P * TC], I32)
        spare = sum1[:, :, :].rearrange("p b d -> p (b d)")[0:STEPS // 2, NT * FILT:]
        dst_2 = spare[:, 0:2 * SE].bitcast(I32).rearrange("p (s e) -> p s e", e=SE)
        rel_2 = spare[:, 2 * SE:3 * SE].bitcast(BF16).rearrange("p (s e) -> p s e", e=SE)
        win_f = sb("win_f", [STEPS // 2, 3, 2])
        win_i = sb("win_i", [STEPS // 2, 2, 2], I32)
        win_s = sb("win_s", [1, 2, STEPS], I32)
        reach = sb("reach", [1, 1])
        is_local = sb("is_local", [1, 1], I32)

        bond_s = sb("bond_s", [P, 2, STEP * BOND])
        z_s = sb("z_s", [P, 2, 512])
        e_s = sb("e_s", [P, 2, 512])
        sp_s = sb("sp_s", [P, 2, 512])
        wt = sb("wt", [P, STEP, FILT])
        rel_s = sb("rel_s", [P, 2, SE // 2], BF16)
        h_win = sb("h_win", [P, 2, P])
        oh_b = sb("oh_b", [P, 2, STEP, BLOCKS], BF16)
        rank_m = sb("rank_m", [P, STEP, BLOCKS])
        pos_f = sb("pos_f", [P, BLOCKS])
        pos_i = sb("pos_i", [P, BLOCKS], I32)
        bits = sb("bits", [P, 3, BLOCKS], I32)
        slot_n = sb("slot_n", [P, 2, STEP], I32)
        slot_i = sb("slot_i", [P, 2, STEP], I32)
        fill_i = sb("fill_i", [P, BLOCKS], I32)
        dst_r = sb("dst_r", [P, 2, STEP], I32)
        rec = sb("rec", [P, 2, STEP, REC])
        rec_meta = rec[:].bitcast(I32)[:, :, :, R_META:R_META + 2]
        cnt = rank_m
        base = sb("base", [P, STEP, BLOCKS])
        blkn = sb("blkn", [P, 8, BLOCKS])
        ntile_i = sb("ntile_i", [P, BLOCKS], I32)
        tabf = sb("tabf", [P, 3, TC])
        tabi = sb("tabi", [P, 3, TC], I32)
        oh_n = sb("oh_n", [P, 2, STEP, P])
        oh_t = sb("oh_t", [P, 2, 512])
        act_s = sb("act_s", [P, 2, 4, HID])
        vg = sb("vg", [P, 2, STEP, HID])
        stat = sb("stat", [P, 5, BLOCKS])
        turned = oh_t[:].rearrange("p u n -> p (u n)")[:, 0:2 * NG * NB].rearrange("p (u n) -> p u n", u=2)
        masks = [v[:].rearrange("p u n -> p (u n)").bitcast(BF16)[:, 0:TILES] for v in (z_s, e_s)]
        blk_bf = sp_s[:].rearrange("p u n -> p (u n)").bitcast(BF16)[:, 0:TILES]
        dst_i = vg[:].rearrange("p u t d -> p (u t d)").bitcast(I32)[:, 0:TILES]
        on_dst = oh_t
        fT_s = oh_n[0:2 * RBF].rearrange("p u t d -> p u (t d)")[:, :, 0:SE // 2]
        hj = act_s[:].rearrange("p u t d -> p (u t d)").rearrange("p (u t f) -> p u t f", u=2, f=FILT)
        six = [rec[:, 0], rec[:, 1], vg[:, 0], vg[:, 1]]
        six += [v[:].rearrange("p u (t c) -> p (u t) c", c=REC) for v in (z_s, e_s)]
        three = [oh_n[:, 0], oh_n[:, 1], act_s[:].rearrange("p u t d -> p (u t) d")]
        blk_i = oh_n[:].rearrange("p u t d -> p (u t d)").bitcast(I32)[:, 0:TILES]
        cmp = act_s[:].rearrange("p u t d -> p (u t d)")[:, 0:TC * BLOCKS].rearrange("p (c b) -> p c b", b=BLOCKS)

        block = ctx.enter_context(nc.Block())

        s_ld = {k: sem("ld_" + k) for k in ("xT", "w", "edges", "xb", "table", "dst_2", "win")}
        WEIGHTS = 19
        s_const, s_pool_const = sem("consts_dve"), sem("consts_pool")

        h_psum, h_sbuf, h_stored = sem("h_psum"), sem("h_sbuf"), sem("h_stored")
        prep = sem("prep")
        oh_ready, oh_used = sem("oh_ready"), sem("oh_used")
        mask_ready, mask_used, cnt_spread = sem("mask_ready"), sem("mask_used"), sem("cnt_spread")
        cnt_ready, bases = sem("cnt_ready"), sem("bases")
        fill_ready, tail_clear, last_clear = sem("fill_ready"), sem("tail_clear"), sem("last_clear")
        tab_ready, tab_stored = sem("tab_ready"), sem("tab_stored")
        ft_in, ft_used, bond_in, bond_used = sems("ft_in"), sem("ft_used"), sems("bond_in"), sem("bond_used")
        dst_ready, hj_in = sem("dst_ready"), sems("hj_in")
        z_ready, zc_ready, ex_ready, ln_ready = sem("z_ready"), sem("zc_ready"), sem("ex_ready"), sem("ln_ready")
        sp_ready, wt_ready = sem("sp_ready"), sem("wt_ready")
        rank_ready, rank_read = sem("rank_ready"), sem("rank_read")
        dve_slot, dve_rec = sem("dve_slot"), sem("dve_rec")
        win_part, win_ready, rel_stored = sem("win_part"), sem("win_ready"), sem("rel_stored")
        path_ready = sem("path_ready")
        rel_in, win_in, on_dst_ready, hj_psum = sems("rel_in"), sems("win_in"), sem("on_dst_ready"), sem("hj_psum")
        slot_ready, rec_dve, rec_act = sem("slot_ready"), sem("rec_dve"), sem("rec_act")
        rec_out = sems("rec_out")
        held = sem("held")
        phase = {k: sem("end_" + k) for k in ("sort", "sum", "node", "edge")}
        rb_in, rb_used = sems("rb_in", 6), sem("rb_used")
        ohn_ready, sum_done, sum0_ready = sem("ohn_ready"), sem("sum_done"), sem("sum0_ready")
        xb_ready, sum1_clear = sem("xb_ready"), sem("sum1_clear")
        n = {k: sem("node_" + k) for k in ("T", "Tc", "z", "zc", "e", "l", "sp", "o", "b2", "add", "mean",
                                           "neg", "sq", "dve", "var", "std", "x1", "T2", "T2c", "uv", "u", "v")}
        out_stored = sem("out_stored")
        wc_in, v_out = sem("wc_in"), sems("v_out")
        rc_in, rc_used = sems("rc_in"), sem("rc_used")
        e = {k: sem("edge_" + k) for k in ("oh", "oh_used", "bond", "T", "Tc", "pre", "add", "silu", "agg", "acc",
                                           "vg_used")}
        vg_in = [sems(f"vg_in{u}_") for u in range(2)]
        f = {k: sem("last_" + k) for k in ("T", "Tc", "y", "add", "mean", "neg", "sq", "dve", "var", "std", "out")}

        def clear_last_tiles(eng, blocks):
            eng.wait_ge(tail_clear, 16 * (SLOT_STEPS - STEPS))
            eng.wait_ge(fill_ready, 1)
            for b in blocks:
                row = eng.value_load(fill_i[0:1, b:b + 1], min_val=0, max_val=SLOTS - SE + STEP - 1)
                eng.dma_start(slots[bass.ds(row, P, step=STEP)], zeros[:, 0:REC]).then_inc(last_clear, 16)

        def sort_path(eng, loop):
            eng.wait_ge(path_ready, 1)
            near = eng.value_load(is_local[0:1, 0:1], min_val=0, max_val=1)
            with eng.If(near == 1):
                loop(True)
            with eng.Else():
                loop(False)

        def pairs(eng, steps, first, step):
            first()
            looped = (steps - 1) // 2
            with eng.Fori(0, looped) as i:
                for u in range(2):
                    step(i * 2 + u, i, u, True)
            for k in range(2 * looped, steps):
                step(k, k // 2, k % 2, k + 1 < steps)

        def rounds(eng, steps, n, step):
            with eng.Fori(0, steps // n) as i:
                for u in range(n):
                    step(i * n + u, i, u)
            for k in range(steps // n * n, steps):
                step(k, k // n, k % n)

        def after(r, u):
            return (r + u, 1 - u)

        def end(eng, name):
            eng.drain().then_inc(phase[name], 1)

        def slot_rows(eng, done, n0, pos, tmp, res):
            eng.tensor_scalar(tmp[0], pos, -SE, None, ALU.bitwise_and).then_inc(done, 1)
            eng.tensor_scalar(tmp[1], pos, P - 1, 3, ALU.bitwise_and, ALU.logical_shift_left).then_inc(done, 1)
            eng.tensor_scalar(tmp[2], pos, 7, STEP - 1, ALU.logical_shift_right, ALU.bitwise_and).then_inc(done, 1)
            eng.wait_ge(done, n0 + 2)
            eng.tensor_tensor(tmp[1], tmp[0], tmp[1], ALU.bitwise_or).then_inc(done, 1)
            eng.wait_ge(done, n0 + 4)
            return eng.tensor_tensor(res, tmp[1], tmp[2], ALU.bitwise_or)

        @block.sync
        def _(sp):
            sp.dma_start(src_i, src).then_inc(s_ld["edges"], 16)
            sp.dma_start(dst_i, dst).then_inc(s_ld["edges"], 16)
            sp.dma_start(w_s[:], weight).then_inc(s_ld["edges"], 16)
            row = lambda v, n: v.rearrange("(a n) -> a n", a=1).broadcast_to([P, n])
            col = lambda v: v.rearrange("(n a) -> n a", a=1)
            loads = [(w_in_s[:], w_in), (b_in_s[:], row(b_in, FILT)), (wf1_s[0:RBF, 0:FILT], w_f1),
                     (wf1_s[RBF:2 * RBF, FILT:P], w_f1),
                     (bf1_s[0:FILT], col(b_f1)), (bf1_s[FILT:P], col(b_f1)),
                     (wf2_s[0:FILT, 0:FILT], w_f2), (wf2_s[FILT:P, FILT:P], w_f2),
                     (bf2_s[:].rearrange("a (t f) -> a t f", f=FILT),
                      b_f2.rearrange("(a t f) -> a t f", a=1, t=1).broadcast_to([1, STEP, FILT])),
                     (wo1_s[0:FILT], w_o1), (wo1_s[FILT:P], w_o1), (bo1_s[:], col(b_o1)),
                     (wo2_s[:], w_o2), (bo2_s[:], row(b_o2, HID)), (b1_s[:], row(b1, HID)),
                     (wab_s[:, 0:HID], W1[0:HID]), (wab_s[:, HID:2 * HID], W1[HID:2 * HID]),
                     (w2_s[:], W2), (b2_s[:], row(b2, HID))]
            assert len(loads) == WEIGHTS
            sp.wait_ge(s_const, 4)
            for to, of in loads:
                sp.dma_start(to, of).then_inc(s_ld["w"], 16)
            sp.dma_start(xT_s, xT).then_inc(s_ld["xT"], 16)
            sp.dma_start(dst_2, dst_steps.rearrange("(p s) e -> p s e", s=2)).then_inc(s_ld["dst_2"], 16)
            sp.dma_start(x_blk[0:NB], xb).then_inc(s_ld["xb"], 16)
            for g in range(STEPS, SLOT_STEPS):
                sp.dma_start(slot_steps[g], zeros[:]).then_inc(tail_clear, 16)
            sp.wait_ge(win_ready, 1)
            sp.dma_start(rel_rows.rearrange("(p s) e -> p s e", s=2), rel_2).then_inc(rel_stored, 16)
            for k in range(2):
                sp.dma_start(win_table[k].rearrange("(p s) -> p s", s=2), win_i[:, k]).then_inc(rel_stored, 16)
            sp.wait_ge(rel_stored, 48)
            sp.dma_start(win_s[:], win_table.rearrange("(a k) s -> a k s", a=1)).then_inc(s_ld["win"], 16)
            for g in range(NT // 7):
                sp.wait_ge(h_sbuf, g + 1)
                sp.dma_start(h_rows.rearrange("(t p) f -> p t f", p=P)[:, 7 * g:7 * g + 7],
                             h_s[:, 7 * g:7 * g + 7]).then_inc(h_stored, 16)
            def sort_loads(local):
                def step(k, r, u):
                    sp.wait_ge(ft_used, k + 1)
                    sp.dma_start(fT_s[:, u], fT[bass.ds(k, 1)].rearrange("a r e -> (a r) e")).then_inc(ft_in[u], 16)
                    if local:
                        at = sp.value_load(win_s[0:1, 0, bass.ds(k, 1)], min_val=0, max_val=NPAD - WIN)
                        sp.wait_ge(on_dst_ready, k + 1)
                        for a in range(2):
                            sp.dma_start(rel_s[a * WIN:(a + 1) * WIN, u], rel_rows[
                                bass.ds(k, 1), a * (SE // 2):(a + 1) * (SE // 2)].broadcast_to(
                                [WIN, SE // 2])).then_inc(rel_in[u], 16)
                        sp.wait_ge(hj_psum, k + 1)
                        for a in range(2):
                            sp.dma_start(h_win[a * WIN:(a + 1) * WIN, u, a * FILT:(a + 1) * FILT],
                                         h_rows[bass.ds(at, WIN)]).then_inc(win_in[u], 16)
                    sp.wait_ge(bond_used, k + 1)
                    sp.dma_start(bond_s[:, u], bond[bass.ds(k, 1)].rearrange("a p e -> (a p) e")).then_inc(
                        bond_in[u], 16)

                step(0, 0, 0)
                step(1, 0, 1)
                clear_last_tiles(sp, range(2 * CLEARS, BLOCKS, 3))
                with sp.Fori(1, STEPS // 2) as i:
                    for u in range(2):
                        step(i * 2 + u, i, u)

            sp.wait_ge(h_stored, 16 * (NT // 7))
            sort_path(sp, sort_loads)

            sp.wait_ge(tab_ready, 1)
            for k in range(2):
                sp.dma_start(tile_table[k].rearrange("(p c) -> p c", c=TC), tabi[:, k]).then_inc(tab_stored, 16)
            sp.wait_ge(tab_stored, 32)
            sp.dma_start(table[:], tile_table).then_inc(s_ld["table"], 16)

            sp.wait_ge(phase["sort"], 4)
            def load_six(k, r, u):
                sp.wait_ge(rb_used, k + 1)
                sp.dma_start(six[u], slot_steps[bass.ds(k, 1)].rearrange(
                    "a p (t c) -> (a p) t c", c=REC)).then_inc(rb_in[u], 16)

            rounds(sp, SLOT_STEPS, 6, load_six)

            sp.wait_ge(phase["sum"], 1)
            wc_rows = W1[2 * HID:2 * HID + BOND].rearrange("r (a d) -> r a d", a=1)
            sp.dma_start(src_w[NB:P], wc_rows.broadcast_to([BOND, BLOCKS, HID])).then_inc(wc_in, 16)
            for g in range(BLOCKS // NG):
                sp.wait_ge(n["v"], g + 1)
                sp.dma_start(v_rows[NG * g * NB:NG * (g + 1) * NB].rearrange("(k n) d -> n k d", n=NB),
                             vg[0:NB, g % 2, 0:NG]).then_inc(v_out[g % 2], 16)

            sp.wait_ge(phase["node"], 3)
            def load_two(k, r, u):
                sp.wait_ge(rc_used, k + 1)
                sp.dma_start(rec[:, u], slot_steps[bass.ds(k, 1)].rearrange(
                    "a p (t c) -> (a p) t c", c=REC)).then_inc(rc_in[u], 16)

            rounds(sp, SLOT_STEPS, 2, load_two)

            full = NODES // NB
            for b in range(0, full, 2 * NG):
                to = min(b + 2 * NG, full)
                sp.wait_ge(f["out"], to)
                sp.dma_start(out[b * NB:to * NB].rearrange("(b n) d -> n b d", n=NB), x_blk[0:NB, b:to]).then_inc(
                    out_stored, 16)
            sp.wait_ge(f["out"], BLOCKS)
            sp.dma_start(out[full * NB:NODES], x_blk[0:NODES - full * NB, full]).then_inc(out_stored, 16)
            sp.wait_ge(out_stored, 16 * (-(-full // (2 * NG)) + 1))

        @block.gpsimd
        def _(pool):
            pool.iota(iota_b[:], [[1, BLOCKS]], base=0, channel_multiplier=0,
                      allow_small_or_imprecise_dtypes=True).then_inc(s_pool_const, 1)
            pool.iota(iota_n[:], [[1, NB]], base=1, channel_multiplier=0,
                      allow_small_or_imprecise_dtypes=True).then_inc(s_pool_const, 1)
            pool.iota(tile_no[:], [[1, TC]], base=0, channel_multiplier=TC,
                      allow_small_or_imprecise_dtypes=True).then_inc(s_pool_const, 1)
            pool.iota(lane[:], [[1, 1]], base=0, channel_multiplier=1,
                      allow_small_or_imprecise_dtypes=True).then_inc(s_pool_const, 1)
            pool.iota(lane_i[:], [[1, 1]], base=0, channel_multiplier=1).then_inc(s_pool_const, 1)
            pool.wait_ge(s_const, 11)
            pool.affine_select(out=before[:], in_=before[:], compare_op=ALU.is_gt, fill=0.0, base=0,
                               pattern=[[1, P]], channel_multiplier=-1).then_inc(s_pool_const, 1)
            pool.affine_select(out=not_before[:], in_=not_before[:], compare_op=ALU.is_ge, fill=0.0, base=0,
                               pattern=[[-1, P]], channel_multiplier=1).then_inc(s_pool_const, 1)
            pool.affine_select(out=ident[:], in_=ident[:], compare_op=ALU.not_equal, fill=1.0, base=0,
                               pattern=[[-1, P]], channel_multiplier=1).then_inc(s_pool_const, 1)

            pool.wait_ge(s_ld["xb"], 16)
            pool.wait_ge(s_ld["w"], 16 * WEIGHTS)
            pool.tensor_tensor(x_blk[0:NB], x_blk[0:NB], bo2_s[0:NB].unsqueeze(1).to_broadcast([NB, BLOCKS, HID]),
                               ALU.add).then_inc(xb_ready, 1)
            pool.wait_ge(h_stored, 16 * (NT // 7))
            pool.wait_ge(rel_stored, 48)
            pool.memset(sum1[:], 0.0).then_inc(sum1_clear, 1)
            pool.wait_ge(tail_clear, 16 * (SLOT_STEPS - STEPS))
            pool.wait_ge(fill_ready, 1)
            pool.sem_inc(held)
            for b in range(2 * CLEARS):
                pool.indirect_dma_start(slots, bass.IndirectOffsetOnAxis(fill_i[:, b:b + 1], 0), zeros[:, 0:REC],
                                        None).then_inc(rec_out[b % 2], 16)
            for u in range(2):
                pool.wait_ge(rec_out[u], 16 * CLEARS)
            pool.wait_ge(last_clear, 16 * (BLOCKS - 2 * CLEARS))

            def sort_moves(local):
                def gather(k, u):
                    pool.wait_ge(dst_ready, k + 1)
                    pool.sem_inc(held)
                    for t in range(STEP):
                        pool.indirect_dma_start(hj[:, u, t], None, h_rows,
                                                bass.IndirectOffsetOnAxis(dst_r[:, u, t:t + 1], 0)).then_inc(
                            hj_in[u], 16)

                def step(k, r, u, more):
                    if more and not local:
                        gather(k + 1, 1 - u)
                    pool.wait_ge(slot_ready, k + 1)
                    pool.wait_ge(rec_act, k + 1)
                    pool.wait_ge(rec_dve, k + 1)
                    pool.sem_inc(held)
                    for t in range(STEP):
                        pool.indirect_dma_start(slots, bass.IndirectOffsetOnAxis(slot_i[:, u, t:t + 1], 0),
                                                rec[:, u, t], None).then_inc(rec_out[u], 16)

                pairs(pool, STEPS, lambda: None if local else gather(0, 0), step)

            sort_path(pool, sort_moves)
            for u in range(2):
                pool.wait_ge(rec_out[u], 16 * (CLEARS + TILES // 2))
            end(pool, "sort")

            for g in range(BLOCKS // NG):
                blocks = slice(NG * g, NG * (g + 1))
                pool.wait_ge(sum0_ready, 1)
                if g >= 1:
                    pool.wait_ge(n["b2"], 2 * g)
                count_b2 = wt[0:NB].rearrange("p t f -> p (t f)").rearrange("p (b d) -> p b d", d=HID)
                pool.tensor_tensor(count_b2, b2_s[0:NB].unsqueeze(1).to_broadcast([NB, NG, HID]),
                                   deg[0:NB, blocks].unsqueeze(2).to_broadcast([NB, NG, HID]), ALU.mult).then_inc(
                    n["b2"], 1)
                pool.wait_ge(n["T2"], g + 1)
                pool.wait_ge(n["b2"], 2 * g + 1)
                pool.tensor_tensor(x_blk[0:NB, blocks], x_blk[0:NB, blocks], count_b2, ALU.add).then_inc(n["b2"], 1)

            for u in range(2):
                pool.wait_ge(v_out[u], 16 * (BLOCKS // NG // 2))
            def gather_v(k, r, u):
                pool.wait_ge(rc_in[u], r * 16 + 16)
                pool.wait_ge(e["vg_used"], k + 1)
                pool.sem_inc(held)
                for t in range(STEP):
                    pool.indirect_dma_start(vg[:, u, t], None, v_rows,
                                            bass.IndirectOffsetOnAxis(rec_meta[:, u, t, 1:2], 0)).then_inc(
                        vg_in[u][t // 4], 16)

            rounds(pool, SLOT_STEPS, 2, gather_v)

        @block.scalar
        def _(act):
            act.sem_inc(bond_used, 2)
            act.preload_act_table_set("natural_log_exp_and_others")
            act.wait_ge(s_const, 1)
            clear_last_tiles(act, (b for b in range(2 * CLEARS, BLOCKS) if (b - 2 * CLEARS) % 3))

            def logs(k, u):
                act.wait_ge(zc_ready, k + 1)
                act.activation(e_s[:, u], z_s[:, u], ACT.Exp).then_inc(ex_ready, 1)
                act.wait_ge(ex_ready, k + 1)
                act.activation(e_s[:, u], e_s[:, u], ACT.Ln, bias=half[:, 0:1], scale=0.5).then_inc(ln_ready, 1)

            def step(k, r, u, more):
                if more:
                    logs(k + 1, 1 - u)
                act.wait_ge(bond_in[u], r * 16 + 16)
                act.wait_ge(rec_out[u], r * P + 16 * CLEARS)
                act.activation(rec[:, u, :, R_BOND:R_BOND + BOND],
                               bond_s[:, u].rearrange("p (t c) -> p t c", c=BOND), ACT.Copy).then_inc(rec_act, 1)
                act.wait_ge(rec_act, k + 1)
                act.sem_inc(bond_used, 1)

            pairs(act, STEPS, lambda: logs(0, 0), step)
            end(act, "sort")

            def squares(p, m):
                act.wait_ge(m["neg"], p + 1)
                if p >= 2:
                    act.wait_ge(m["sq"], NG * (p - 1))
                for j in range(NG):
                    b = NG * p + j
                    act.activation(act_s[0:NB, p % 2, j], x_blk[0:NB, b], ACT.Square, bias=stat[0:NB, 4, b:b + 1],
                                   accum_out=stat[0:NB, 1, b:b + 1]).then_inc(m["sq"], 1)

            G = BLOCKS // NG
            def turned_sums(g):
                act.wait_ge(n["T"], g + 1)
                act.activation(turned[:, g % 2, 0:2 * NB], ps[:, g % 2, 0:2 * NB], ACT.Copy).then_inc(n["Tc"], 1)

            turned_sums(0)
            for g in range(G + 3):
                if g + 1 < G:
                    turned_sums(g + 1)
                if g < G:
                    act.wait_ge(n["zc"], g + 1)
                    act.activation(e_s[:, g % 2, 0:NG * NB], z_s[:, g % 2, 0:NG * NB], ACT.Exp).then_inc(n["e"], 1)
                    act.wait_ge(n["e"], g + 1)
                    act.activation(e_s[:, g % 2, 0:NG * NB], e_s[:, g % 2, 0:NG * NB], ACT.Ln, bias=half[:, 0:1],
                                   scale=0.5).then_inc(n["l"], 1)
                if g >= 3:
                    squares(g - 3, n)
            act.wait_ge(n["var"], 1)
            act.activation(stat[0:NB, 2], stat[0:NB, 1], ACT.Sqrt).then_inc(n["std"], 1)
            for g in range(G + 2):
                if g < G:
                    act.wait_ge(n["T2"], g + 1)
                    act.activation(turned[:, g % 2], ps[:, 4 + g % 2, 0:NG * NB], ACT.Copy).then_inc(n["T2c"], 1)
                if g >= 2:
                    p = g - 2
                    act.wait_ge(n["uv"], p + 1)
                    if p >= 2:
                        act.wait_ge(v_out[p % 2], 16 * (p // 2))
                    act.activation(vg[0:NB, p % 2, 0:NG], ps[0:NB, p % 2 * 2 + 1].rearrange("p (b d) -> p b d", d=HID),
                                   ACT.Copy).then_inc(n["v"], 1)
            end(act, "node")

            act.wait_ge(phase["node"], 3)
            for u in range(2):
                act.wait_ge(v_out[u], 16 * (BLOCKS // NG // 2))
            act.preload_act_table(ACT.Silu)

            def turn(k, r, u):
                act.wait_ge(rc_in[u], r * 16 + 16)
                act.wait_ge(e["oh_used"], k + 1)
                act.activation(oh_n[:, u, :, NB:P], rec[:, u, :, R_BOND:R_BOND + BOND], ACT.Copy).then_inc(
                    e["bond"], 1)
                for q in range(2):
                    act.wait_ge(e["T"], k * 2 + (q + 1))
                    act.activation(oh_t[:, q], ps[:, q], ACT.Copy).then_inc(e["Tc"], 1)

            def step(k, r, u, more):
                for q in range(2):
                    act.wait_ge(e["add"], k * 2 + (q + 1))
                    act.activation(act_s[:, q], vg[:, u, 4 * q:4 * q + 4], ACT.Silu).then_inc(e["silu"], 1)
                act.wait_ge(e["silu"], k * 2 + 2)
                act.sem_inc(e["vg_used"], 1)
                if more:
                    turn(k + 1, *after(r, u))

            pairs(act, SLOT_STEPS, lambda: turn(0, 0, 0), step)
            end(act, "edge")

            for g in range(G + 3):
                if g < G:
                    act.wait_ge(f["T"], g + 1)
                    act.activation(turned[:, g % 2], ps[:, g % 2, 0:NG * NB], ACT.Copy).then_inc(f["Tc"], 1)
                if g >= 3:
                    squares(g - 3, f)
            act.wait_ge(f["var"], 1)
            act.activation(stat[0:NB, 2], stat[0:NB, 1], ACT.Sqrt).then_inc(f["std"], 1)

        @block.tensor
        def _(pe):
            pe.sem_inc(ft_used, 2)
            pe.sem_inc(oh_used, 2)
            pe.sem_inc(mask_used, 2)
            pe.sem_inc(rb_used, 6)
            pe.wait_ge(s_const, 11)
            pe.wait_ge(s_pool_const, 8)
            pe.matmul(ps[:, 2, 0:BLOCKS], zeros[:, 0:P], zeros[:, 0:BLOCKS], start=True, stop=True)
            for g in range(PARTS):
                with pe.Fori(0, BLOCKS // PARTS // 4) as i:
                    for u in range(4):
                        b = i * 4 + (g * (BLOCKS // PARTS) + u)
                        pe.wait_ge(mask_ready, b + 1)
                        for c in range(0, TILES, P):
                            m = min(P, TILES - c)
                            mm = pe.matmul(ps[0:m, 2, bass.ds(b, 1)], masks[u % 2][:, c:c + m], ones_bf[:, 0:1],
                                           start=False, stop=True, skip_group_check=True)
                        mm.then_inc(mask_used, 1)
                if g == 0:
                    pe.wait_ge(s_ld["w"], 16 * WEIGHTS)
                    pe.wait_ge(s_ld["xT"], 16)
                if g >= 2:
                    pe.wait_ge(h_sbuf, g - 1)
                for t in range(7):
                    nodes = slice((7 * g + t) * P, (7 * g + t + 1) * P)
                    mm = pe.matmul(ps[:, g % 2, t * FILT:(t + 1) * FILT], xT_s[:, nodes], w_in_s[:],
                                   start=True, stop=True)
                mm.then_inc(h_psum, 1)
            pe.wait_ge(mask_used, 2 + BLOCKS)
            pe.sem_inc(cnt_ready, 1)
            pe.wait_ge(cnt_spread, 1)
            pe.matmul(ps[:, 3, 0:STEP * BLOCKS], ones[:], cnt[:].rearrange("p t b -> p (t b)"), start=True,
                      stop=True).then_inc(cnt_ready, 1)

            run = ps[:, 4, 0:STEP * BLOCKS]
            pe.wait_ge(bases, 1)
            pe.matmul(run, ident[:], base[:].rearrange("p t b -> p (t b)"), start=True, stop=True)

            def sort_products(local):
                def filt(k, r, u):
                    pe.wait_ge(ft_in[u], r * 16 + 16)
                    pe.matmul(ps[:, u], wf1_s[:], fT_s[:, u], start=True, stop=True).then_inc(z_ready, 1)
                    pe.wait_ge(z_ready, k + 1)
                    pe.sem_inc(ft_used, 1)

                def rank(k, u):
                    pe.wait_ge(oh_ready, k + 1)
                    pe.matmul(run, before[:], oh_b[:, u].rearrange("p t b -> p (t b)"), start=False, stop=True,
                              skip_group_check=True).then_inc(rank_ready, 1)

                def whole(k, u):
                    pe.wait_ge(rank_read, k + 1)
                    pe.matmul(run, not_before[:], oh_b[:, u].rearrange("p t b -> p (t b)"), start=False, stop=True,
                              skip_group_check=True).then_inc(oh_used, 1)

                def first():
                    if local:
                        pe.sem_inc(hj_psum, 2)
                    filt(0, 0, 0)
                    filt(1, 0, 1)
                    rank(0, 0)
                    whole(0, 0)

                def step(k, r, u, more, filt_too=True):
                    if local:
                        pe.wait_ge(win_in[u], r * 32 + 32)
                        pe.wait_ge(on_dst_ready, k + 3)
                        for j in range(4):
                            mm = pe.matmul(ps[:, 5 + u, j * P:(j + 1) * P], on_dst[:, u, j * P:(j + 1) * P],
                                           h_win[:, u], start=True, stop=True)
                        mm.then_inc(hj_psum, 1)
                    pe.wait_ge(sp_ready, k + 1)
                    pe.matmul(ps[:, 2 + u], ones[0:1], bf2_s[:], start=True, stop=True)
                    for j in range(4):
                        mm = pe.matmul(ps[:, 2 + u, j * P:(j + 1) * P], sp_s[:, u, j * P:(j + 1) * P], wf2_s[:],
                                       start=False, stop=True, skip_group_check=True)
                    mm.then_inc(wt_ready, 1)
                    if more:
                        rank(k + 1, 1 - u)
                        if filt_too:
                            filt(k + 2, r + 1, u)
                        whole(k + 1, 1 - u)

                first()
                with pe.Fori(0, STEPS // 2 - 1) as i:
                    for u in range(2):
                        step(i * 2 + u, i, u, True)
                step(STEPS - 2, STEPS // 2 - 1, 0, True, filt_too=False)
                step(STEPS - 1, STEPS // 2 - 1, 1, False)

            sort_path(pe, sort_products)
            end(pe, "sort")

            pe.wait_ge(s_ld["table"], 16)
            pe.wait_ge(phase["sort"], 4)
            for k in range(BANKS):
                pe.matmul(ps[:, k], zeros[:, 0:P], zeros[:, 0:512], start=True, stop=True)
            flat = ps[:].rearrange("p k n -> p (k n)")
            def add_step(k, r, u):
                _, at = nc.values_load_multi_w_load_instructions(
                    table[1:2, bass.ds(k * STEP, STEP)], PE_ONLY, min_val=0,
                    max_val=(BANKS - 1) * 512 + (PER_BANK - 1) * MSG,
                    skip_runtime_bounds_check_because="clamped to the last block when the table is made")
                pe.wait_ge(rb_in[u], r * 16 + 16)
                pe.wait_ge(ohn_ready, k + 1)
                for t in range(STEP):
                    mm = pe.matmul(flat[0:NB, bass.ds(at[t], WIDE)], three[u % 3][:, t, 0:NB], six[u][:, t, 0:WIDE],
                                   start=False, stop=True, skip_group_check=True)
                mm.then_inc(rb_used, 1)

            rounds(pe, SLOT_STEPS, 6, add_step)
            pe.wait_ge(rb_used, 6 + SLOT_STEPS)
            pe.sem_inc(sum_done, 1)

            pe.wait_ge(sum0_ready, 1)
            G = BLOCKS // NG
            for g in range(G + 2):
                if g < G:
                    for q in range(2):
                        b = NG * g + 2 * q
                        mm = pe.transpose(ps[:, g % 2, q * NB:(q + 1) * NB],
                                          sum0[0:NB, b:b + 2].rearrange("p b f -> p (b f)"), ident[0:NB, 0:NB])
                    mm.then_inc(n["T"], 1)
                if 1 <= g <= G:
                    p = g - 1
                    pe.wait_ge(n["Tc"], p + 1)
                    for j in range(NG):
                        half_ = slice(FILT * (j % 2), FILT * (j % 2) + FILT)
                        mm = pe.matmul(ps[:, 2 + 4 * (p % 2) + j % 2, j // 2 * NB:(j // 2 + 1) * NB], wo1_s[half_, :],
                                       turned[half_, p % 2, j // 2 * NB:(j // 2 + 1) * NB], start=True, stop=True)
                    mm.then_inc(n["z"], 1)
                if g >= 2:
                    p = g - 2
                    pe.wait_ge(n["sp"], p + 1)
                    if p >= 2:
                        pe.wait_ge(n["add"], p - 1)
                    for j in range(NG):
                        at_ = j % 2 * (NG // 2) + j // 2
                        mm = pe.matmul(ps[0:NB, 4 + p % 2, j * HID:(j + 1) * HID],
                                       sp_s[:, p % 2, at_ * NB:(at_ + 1) * NB], wo2_s[:], start=True, stop=True)
                    mm.then_inc(n["o"], 1)
            for g in range(G + 1):
                if g < G:
                    pe.wait_ge(n["x1"], NG * (g + 1))
                    for j in range(NG):
                        mm = pe.transpose(ps[:, 4 + g % 2, j * NB:(j + 1) * NB], x_blk[0:NB, NG * g + j],
                                          ident[0:NB, 0:NB])
                    mm.then_inc(n["T2"], 1)
                if g >= 1:
                    p = g - 1
                    pe.wait_ge(n["T2c"], p + 1)
                    if p >= 2:
                        pe.wait_ge(n["u"], p - 1)
                        pe.wait_ge(n["v"], p - 1)
                    for j in range(NG):
                        for k in range(2):
                            mm = pe.matmul(ps[0:NB, p % 2 * 2 + k, j * HID:(j + 1) * HID],
                                           turned[:, p % 2, j * NB:(j + 1) * NB], wab_s[:, k * HID:(k + 1) * HID],
                                           start=True, stop=True)
                    mm.then_inc(n["uv"], 1)
            end(pe, "node")

            pe.wait_ge(phase["node"], 3)
            pe.wait_ge(wc_in, 16)
            src_flat = src_w[:].rearrange("p b d -> p (b d)")

            def block_rows(k):
                _, at = nc.values_load_multi_w_load_instructions(
                    table[0:1, bass.ds(k * STEP, STEP)], PE_ONLY, min_val=0, max_val=(BLOCKS - 1) * HID,
                    skip_runtime_bounds_check_because="clamped to the last block when the table is made")
                return at

            def spread(k, u, at):
                pe.wait_ge(e["oh"], k + 1)
                pe.wait_ge(e["bond"], k + 1)
                for q in range(2):
                    for t in range(4):
                        mm = pe.transpose(ps[:, q, t * P:(t + 1) * P], oh_n[:, u, 4 * q + t], ident[:])
                    mm.then_inc(e["T"], 1)
                for q in range(2):
                    pe.wait_ge(e["Tc"], k * 2 + (q + 1))
                    for t in range(4):
                        mm = pe.matmul(ps[:, 2 + 2 * u + q, t * HID:(t + 1) * HID], oh_t[:, q, t * P:(t + 1) * P],
                                       src_flat[:, bass.ds(at[4 * q + t], HID)], start=True, stop=True)
                    mm.then_inc(e["pre"], 1)

            def step(k, r, u, more):
                if more:
                    at = block_rows(k + 1)
                for q in range(2):
                    pe.wait_ge(e["silu"], k * 2 + (q + 1))
                    pe.wait_ge(e["acc"], k * 8 + 4 * (q + 1))
                    for t in range(4):
                        mm = pe.matmul(ps[0:NB, 6 + q, t * HID:(t + 1) * HID], oh_n[:, u, 4 * q + t, 0:NB],
                                       act_s[:, q, t], start=True, stop=True)
                    mm.then_inc(e["agg"], 1)
                pe.wait_ge(e["agg"], k * 2 + 2)
                pe.sem_inc(e["oh_used"], 1)
                if more:
                    spread(k + 1, 1 - u, at)

            pairs(pe, SLOT_STEPS, lambda: spread(0, 0, block_rows(0)), step)
            end(pe, "edge")

            pe.wait_ge(phase["edge"], 3)
            for g in range(G + 1):
                if g < G:
                    for j in range(NG):
                        mm = pe.transpose(ps[:, g % 2, j * NB:(j + 1) * NB], sum1[0:NB, NG * g + j],
                                          ident[0:NB, 0:NB])
                    mm.then_inc(f["T"], 1)
                if g >= 1:
                    p = g - 1
                    pe.wait_ge(f["Tc"], p + 1)
                    if p >= 2:
                        pe.wait_ge(f["add"], p - 1)
                    for j in range(NG):
                        mm = pe.matmul(ps[0:NB, 2 + p % 2, j * HID:(j + 1) * HID],
                                       turned[:, p % 2, j * NB:(j + 1) * NB], w2_s[:], start=True, stop=True)
                    mm.then_inc(f["y"], 1)

        @block.vector
        def _(dve):
            for to, v in ((zeros, 0.0), (wf1_s, 0.0), (wf2_s, 0.0), (h_win, 0.0), (ones_bf, 1.0), (before, 1.0),
                          (not_before, 1.0), (ident, 0.0), (half, 0.5), (ones, 1.0), (rec, 0.0)):
                dve.memset(to[:], v).then_inc(s_const, 1)
            dve.wait_ge(s_const, 11)
            dve.memset(rec[:, :, :, R_ONE:R_ONE + 1], 1.0).then_inc(s_const, 1)

            dve.wait_ge(s_ld["edges"], 48)
            dve.tensor_scalar(blk_i, src_i, 1.0 / NB, 0.5 / NB - 0.5, ALU.mult, ALU.add).then_inc(prep, 1)
            dve.tensor_scalar(src_1, src_i, 1.0, None, ALU.add).then_inc(prep, 1)
            dve.tensor_copy(meta[:, :, 1], dst_i).then_inc(prep, 1)
            dve.wait_ge(prep, 1)
            dve.tensor_copy(blk_f[:], blk_i).then_inc(prep, 1)
            dve.tensor_copy(blk_bf, blk_i).then_inc(prep, 1)
            dve.wait_ge(prep, 5)
            dve.scalar_tensor_tensor(out=meta[:, :, 0], in0=blk_f[:], scalar=-float(NB), in1=src_1, op0=ALU.mult,
                                     op1=ALU.add).then_inc(prep, 1)
            dve.wait_ge(s_ld["w"], 16 * WEIGHTS)
            dve.tensor_scalar(bf1_l[:], bf1_s[:], -LOG2, None, ALU.add).then_inc(prep, 1)
            dve.tensor_scalar(bo1_l[:], bo1_s[:], -LOG2, None, ALU.add).then_inc(prep, 1)

            def more_h(g):
                dve.wait_ge(h_psum, g + 1)
                dve.tensor_tensor(h_s[:, 7 * g:7 * g + 7], ps[:, g % 2, 0:7 * FILT].rearrange("p (t f) -> p t f", f=FILT),
                                  b_in_s[:].unsqueeze(1).to_broadcast([P, 7, FILT]), ALU.add).then_inc(h_sbuf, 1)

            def one_hot_block(k, u):
                return dve.tensor_tensor(oh_b[:, u], blk_f[:, bass.ds(k * STEP, STEP)].unsqueeze(2).to_broadcast(
                    [P, STEP, BLOCKS]), iota_b[:].unsqueeze(1).to_broadcast([P, STEP, BLOCKS]), ALU.is_equal)

            def windows():
                dve.wait_ge(s_ld["dst_2"], 16)
                dve.tensor_reduce(win_f[:, 0], dst_2, X, ALU.min).then_inc(win_part, 1)
                dve.tensor_reduce(win_f[:, 1], dst_2, X, ALU.max).then_inc(win_part, 1)
                dve.wait_ge(win_part, 2)
                dve.tensor_scalar(win_f[:, 2], win_f[:, 0], float(NPAD - WIN), None, ALU.min).then_inc(win_part, 1)
                dve.wait_ge(win_part, 3)
                dve.tensor_copy(win_i[:, 0], win_f[:, 2])
                dve.tensor_tensor(win_i[:, 1], win_f[:, 1], win_f[:, 2], ALU.subtract)
                for k in range(2):
                    last = dve.tensor_scalar(rel_2[:, k], dst_2[:, k], win_f[:, 2, k:k + 1], None, ALU.subtract)
                last.then_inc(win_ready, 1)

            dve.wait_ge(s_pool_const, 8)
            dve.wait_ge(prep, 8)
            for g in range(PARTS):
                with dve.Fori(0, BLOCKS // PARTS // 4) as i:
                    for u in range(4):
                        b = i * 4 + (g * (BLOCKS // PARTS) + u)
                        dve.wait_ge(mask_used, b + 1)
                        dve.tensor_scalar(masks[u % 2], blk_bf, iota_b[:, bass.ds(b, 1)], None,
                                          ALU.is_equal).then_inc(mask_ready, 1)
                if g == 2:
                    windows()
                if g >= 1:
                    more_h(g - 1)
            more_h(PARTS - 1)
            dve.tensor_scalar(lane_half[0:WIN], lane[0:WIN], 0.0, None, ALU.add)
            dve.tensor_scalar(lane_half[WIN:P], lane[WIN:P], -float(WIN), None, ALU.add).then_inc(win_part, 1)

            dve_n = [0]

            def link(ins, s=n["dve"]):
                dve_n[0] += 1
                ins.then_inc(s, 1)
                dve.wait_ge(s, dve_n[0])

            total, ntile, end_t, start_t, one, last_t, pos_b = (blkn[:, j] for j in range(7))
            dve.wait_ge(cnt_ready, 1)
            link(dve.tensor_copy(tile_cnt[:], ps[:, 2, 0:BLOCKS]))
            link(dve.tensor_scalar(lane_i[:], lane_i[:], STEP - 1, None, ALU.bitwise_and))
            link(dve.tensor_copy(blkn[:, 7, 0:1], lane_i[:]))
            link(dve.tensor_scalar(lane_8[:], iota_b[:, 0:STEP], blkn[:, 7, 0:1], None, ALU.is_equal))
            link(dve.tensor_tensor(cnt[:], lane_8[:].unsqueeze(2).to_broadcast([P, STEP, BLOCKS]),
                                   tile_cnt[:].unsqueeze(1).to_broadcast([P, STEP, BLOCKS]), ALU.mult))
            dve.sem_inc(cnt_spread, 1)
            dve.wait_ge(cnt_ready, 2)
            link(dve.tensor_copy(cnt[:], ps[:, 3, 0:STEP * BLOCKS].rearrange("p (t b) -> p t b", b=BLOCKS)))
            link(dve.tensor_reduce(total, cnt[:].rearrange("p t b -> p b t"), X, ALU.add))
            link(dve.tensor_scalar(ntile_i[:], total, 1.0 / P, (P - 1) / 2.0 / P, ALU.mult, ALU.add))
            link(dve.memset(one, 1.0))
            link(dve.tensor_copy(ntile, ntile_i[:]))
            link(dve.tensor_tensor_scan(end_t, one, ntile, 0.0, ALU.mult, ALU.add))
            link(dve.tensor_tensor(start_t, end_t, ntile, ALU.subtract))
            link(dve.tensor_scalar(base[:, 0], start_t, float(P), None, ALU.mult))
            for t in range(1, STEP):
                link(dve.tensor_tensor(base[:, t], base[:, t - 1], cnt[:, t - 1], ALU.add))
            dve.sem_inc(bases, 1)
            link(dve.tensor_scalar(last_t, end_t, -1.0, 0.0, ALU.add, ALU.max))
            link(dve.tensor_scalar(pos_b, last_t, float(P), lane[:, 0:1], ALU.mult, ALU.add))
            link(dve.tensor_copy(pos_i[:], pos_b))
            link(slot_rows(dve, prep, 8, pos_i[:], [bits[:, j] for j in range(3)], fill_i[:]))
            dve.sem_inc(fill_ready, 1)
            dve.wait_ge(s_ld["win"], 16)
            link(dve.tensor_reduce(reach[:], win_s[:, 1], X, ALU.max))
            link(dve.tensor_scalar(is_local[:], reach[:], float(WIN - 1), None, ALU.is_le))
            dve.sem_inc(path_ready, 1)
            link(dve.tensor_tensor(cmp, tile_no[:].unsqueeze(2).to_broadcast([P, TC, BLOCKS]),
                                   end_t.unsqueeze(1).to_broadcast([P, TC, BLOCKS]), ALU.is_ge))
            link(dve.tensor_reduce(tabf[:, 0], cmp, X, ALU.add))
            link(dve.tensor_scalar(tabf[:, 0], tabf[:, 0], float(BLOCKS - 1), None, ALU.min))
            link(dve.tensor_scalar(tabi[:, 2], tabf[:, 0], 1.0 / PER_BANK, 0.5 / PER_BANK - 0.5, ALU.mult, ALU.add))
            link(dve.tensor_copy(tabf[:, 1], tabi[:, 2]))
            link(dve.tensor_scalar(tabf[:, 2], tabf[:, 0], float(MSG), None, ALU.mult))
            link(dve.tensor_scalar(tabi[:, 0], tabf[:, 0], float(HID), None, ALU.mult))
            link(dve.scalar_tensor_tensor(out=tabi[:, 1], in0=tabf[:, 1], scalar=float(512 - PER_BANK * MSG),
                                          in1=tabf[:, 2], op0=ALU.mult, op1=ALU.add))
            dve.sem_inc(tab_ready, 1)

            dve.wait_ge(win_part, 4)

            SLOT_LINKS, REC_LINKS = 7, 3

            def sort_vectors(local):
                def first_half(k, r, u):
                    dve.wait_ge(oh_used, k + 1)
                    one_hot_block(k, u).then_inc(oh_ready, 1)
                    dve.wait_ge(z_ready, k + 1)
                    dve.tensor_scalar(z_s[:, u], ps[:, u], bf1_s[:, 0:1], CAP, ALU.add, ALU.min).then_inc(zc_ready, 1)
                    if local:
                        dve.wait_ge(rel_in[u], r * 32 + 32)
                        dve.wait_ge(hj_psum, k + 1)
                        dve.tensor_scalar(on_dst[:, u], rel_s[:, u], lane_half[:, 0:1], None,
                                          ALU.is_equal).then_inc(on_dst_ready, 1)
                    else:
                        dve.tensor_copy(dst_r[:, u], meta[:, bass.ds(k * STEP, STEP), 1]).then_inc(dst_ready, 1)

                def rank(k, u):
                    dve.wait_ge(rank_ready, k + 1)
                    dve.tensor_tensor(rank_m[:], ps[:, 4, 0:STEP * BLOCKS].rearrange("p (t b) -> p t b", b=BLOCKS),
                                      oh_b[:, u], ALU.mult).then_inc(rank_read, 1)

                def slot(k, u):
                    done = k * SLOT_LINKS
                    dve.wait_ge(rank_read, k + 1)
                    dve.tensor_reduce(pos_f[:, 0:STEP], rank_m[:], X, ALU.add).then_inc(dve_slot, 1)
                    dve.wait_ge(dve_slot, done + 1)
                    dve.tensor_copy(pos_i[:, 0:STEP], pos_f[:, 0:STEP]).then_inc(dve_slot, 1)
                    dve.wait_ge(dve_slot, done + 2)
                    slot_rows(dve, dve_slot, done + 2, pos_i[:, 0:STEP], [bits[:, j, 0:STEP] for j in range(3)],
                              slot_n[:, u]).then_inc(dve_slot, 1)

                def softplus(k, u):
                    dve.wait_ge(ln_ready, k + 1)
                    dve.scalar_tensor_tensor(out=sp_s[:, u], in0=ps[:, u], scalar=bf1_l[:, 0:1], in1=e_s[:, u],
                                             op0=ALU.add, op1=ALU.max).then_inc(sp_ready, 1)

                def first():
                    if local:
                        dve.sem_inc(on_dst_ready, 2)
                    first_half(0, 0, 0)
                    rank(0, 0)
                    slot(0, 0)
                    softplus(0, 0)

                def step(k, r, u, more):
                    if more:
                        first_half(k + 1, *after(r, u))
                    halves = lambda v: v.rearrange("p (j a f) -> p a j f", a=2, f=FILT)
                    dve.wait_ge(wt_ready, k + 1)
                    dve.tensor_tensor(wt[:].rearrange("p (a j) f -> p a j f", a=2), halves(ps[:, 2 + u]),
                                      w_s[:, bass.ds(k * STEP, STEP)].rearrange("p (a j) -> p a j", a=2).unsqueeze(
                                          3).to_broadcast([P, 2, 4, FILT]), ALU.mult).then_inc(dve_rec, 1)
                    if more:
                        rank(k + 1, 1 - u)
                    dve.wait_ge(rec_out[u], r * P + 16 * CLEARS)
                    dve.wait_ge(dve_slot, k * SLOT_LINKS + SLOT_LINKS)
                    dve.tensor_copy(slot_i[:, u], slot_n[:, u]).then_inc(slot_ready, 1)
                    dve.tensor_copy(rec_meta[:, u], meta[:, bass.ds(k * STEP, STEP), :]).then_inc(dve_rec, 1)
                    dve.wait_ge(dve_rec, k * REC_LINKS + 1)
                    if local:
                        dve.wait_ge(hj_psum, k + 3)
                        dve.tensor_tensor(rec[:, u, :, 0:FILT].rearrange("p (a j) f -> p a j f", a=2),
                                          wt[:].rearrange("p (a j) f -> p a j f", a=2), halves(ps[:, 5 + u]),
                                          ALU.mult).then_inc(dve_rec, 1)
                    else:
                        dve.wait_ge(hj_in[u], r * P + P)
                        dve.tensor_tensor(rec[:, u, :, 0:FILT], wt[:], hj[:, u], ALU.mult).then_inc(dve_rec, 1)
                    if more:
                        slot(k + 1, 1 - u)
                    dve.wait_ge(dve_rec, k * REC_LINKS + REC_LINKS)
                    dve.sem_inc(rec_dve, 1)
                    if more:
                        softplus(k + 1, 1 - u)

                pairs(dve, STEPS, first, step)

            sort_path(dve, sort_vectors)
            end(dve, "sort")

            def one_hot_node(to, of):
                place = of.bitcast(I32)[:, :, R_META:R_META + 1]
                return dve.tensor_tensor(to[:, :, 0:NB], place.to_broadcast([P, STEP, NB]),
                                         iota_n[:].unsqueeze(1).to_broadcast([P, STEP, NB]), ALU.is_equal)

            def one_hot_step(k, r, u):
                dve.wait_ge(rb_in[u], r * 16 + 16)
                dve.wait_ge(rb_used, k + 4)
                one_hot_node(three[u % 3], six[u]).then_inc(ohn_ready, 1)

            rounds(dve, SLOT_STEPS, 6, one_hot_step)
            dve.wait_ge(sum_done, 1)
            for k in range(BANKS):
                sums = ps[0:NB, k, 0:PER_BANK * MSG].rearrange("p (b f) -> p b f", f=MSG)
                dve.tensor_copy(sum0[0:NB, PER_BANK * k:PER_BANK * (k + 1)], sums[:, :, 0:FILT])
                last = dve.tensor_copy(deg[0:NB, PER_BANK * k:PER_BANK * (k + 1)], sums[:, :, FILT])
            last.then_inc(sum0_ready, 1)
            end(dve, "sum")

            G = BLOCKS // NG
            dve.wait_ge(xb_ready, 1)

            def add(p, bank, m):
                dve.tensor_tensor(x_blk[0:NB, NG * p:NG * (p + 1)], x_blk[0:NB, NG * p:NG * (p + 1)],
                                  ps[0:NB, bank].rearrange("p (b d) -> p b d", d=HID), ALU.add).then_inc(m["add"], 1)

            def mean(p, m):
                dve.wait_ge(m["add"], p + 1)
                blocks = slice(NG * p, NG * (p + 1))
                dve.tensor_reduce(stat[0:NB, 0, blocks], x_blk[0:NB, blocks], X, ALU.add).then_inc(m["mean"], 1)

            def less_mean(p, m):
                dve.wait_ge(m["mean"], p + 1)
                blocks = slice(NG * p, NG * (p + 1))
                dve.tensor_scalar(stat[0:NB, 4, blocks], stat[0:NB, 0, blocks], -1.0 / HID, None, ALU.mult).then_inc(
                    m["neg"], 1)

            def deviation(m):
                dve.wait_ge(m["sq"], BLOCKS)
                dve.tensor_scalar(stat[0:NB, 1], stat[0:NB, 1], 1.0 / HID, EPS, ALU.mult, ALU.add).then_inc(
                    m["var"], 1)
                dve.wait_ge(m["std"], 1)
                link(dve.reciprocal(stat[0:NB, 3], stat[0:NB, 2]), m["dve"])

            def scale(g, done):
                for b in range(NG * g, NG * (g + 1)):
                    dve.tensor_scalar(x_blk[0:NB, b], x_blk[0:NB, b], stat[0:NB, 4, b:b + 1], stat[0:NB, 3, b:b + 1],
                                      ALU.add, ALU.mult).then_inc(done, 1)

            for g in range(G + 2):
                if g < G:
                    dve.wait_ge(n["z"], g + 1)
                    z = ps[:, 2 + 4 * (g % 2):4 + 4 * (g % 2), 0:2 * NB]
                    both = lambda v: v[:, g % 2, 0:NG * NB].rearrange("p (a n) -> p a n", a=2)
                    dve.tensor_scalar(both(z_s), z, bo1_s[:, 0:1], CAP, ALU.add, ALU.min).then_inc(n["zc"], 1)
                if 1 <= g <= G:
                    dve.wait_ge(n["o"], g)
                    add(g - 1, 4 + (g - 1) % 2, n)
                if g >= 2:
                    less_mean(g - 2, n)
                if 1 <= g <= G:
                    mean(g - 1, n)
                if g < G:
                    dve.wait_ge(n["l"], g + 1)
                    dve.scalar_tensor_tensor(out=both(sp_s), in0=z, scalar=bo1_l[:, 0:1], in1=both(e_s), op0=ALU.add,
                                             op1=ALU.max).then_inc(n["sp"], 1)
            deviation(n)
            for g in range(G + 2):
                if g < G:
                    scale(g, n["x1"])
                if g >= 2:
                    p = g - 2
                    dve.wait_ge(n["uv"], p + 1)
                    dve.tensor_tensor(src_w[0:NB, NG * p:NG * (p + 1)],
                                      ps[0:NB, p % 2 * 2].rearrange("p (b d) -> p b d", d=HID),
                                      b1_s[0:NB].unsqueeze(1).to_broadcast([NB, NG, HID]), ALU.add).then_inc(n["u"], 1)
            end(dve, "node")

            dve.wait_ge(phase["node"], 3)
            dve.wait_ge(sum1_clear, 1)
            dve.sem_inc(rc_used, 2)
            dve.sem_inc(e["oh_used"], 2)
            dve.sem_inc(e["vg_used"], 2)
            dve.sem_inc(e["acc"], 8)
            sum_flat = sum1[:].rearrange("p b d -> p (b d)")

            def one_hot(k, r, u):
                dve.wait_ge(rc_in[u], r * 16 + 16)
                dve.wait_ge(e["oh_used"], k + 1)
                one_hot_node(oh_n[:, u], rec[:, u]).then_inc(e["oh"], 1)

            def step(k, r, u, more):
                _, at = nc.values_load_multi_w_load_instructions(
                    table[0:1, bass.ds(k * STEP, STEP)], DVE_ONLY, min_val=0, max_val=(BLOCKS - 1) * HID,
                    skip_runtime_bounds_check_because="clamped to the last block when the table is made")
                for q in range(2):
                    dve.wait_ge(vg_in[u][q], r * 64 + 64)
                    dve.wait_ge(e["pre"], k * 2 + (q + 1))
                    rows = vg[:, u, 4 * q:4 * q + 4]
                    dve.tensor_tensor(rows, rows, ps[:, 2 + 2 * u + q].rearrange("p (t d) -> p t d", d=HID),
                                      ALU.add).then_inc(e["add"], 1)
                dve.wait_ge(e["bond"], k + 1)
                dve.sem_inc(rc_used, 1)
                if more:
                    one_hot(k + 1, *after(r, u))
                for q in range(2):
                    dve.wait_ge(e["agg"], k * 2 + (q + 1))
                    for t in range(4):
                        dve.wait_ge(e["acc"], k * 8 + (4 * q + t + 8))
                        here = sum_flat[0:NB, bass.ds(at[4 * q + t], HID)]
                        dve.tensor_tensor(here, here, ps[0:NB, 6 + q, t * HID:(t + 1) * HID], ALU.add).then_inc(
                            e["acc"], 1)

            pairs(dve, SLOT_STEPS, lambda: one_hot(0, 0, 0), step)
            end(dve, "edge")

            dve_n[0] = 0
            dve.wait_ge(n["b2"], 2 * (BLOCKS // NG))
            for g in range(G + 2):
                if 1 <= g <= G:
                    dve.wait_ge(f["y"], g)
                    add(g - 1, 2 + (g - 1) % 2, f)
                if g >= 2:
                    less_mean(g - 2, f)
                if 1 <= g <= G:
                    mean(g - 1, f)
            deviation(f)
            for g in range(G):
                scale(g, f["out"])


_OUT = ((NODES, HID), np.float32)


def kernel(**inputs):
    import concourse.bacc as bacc
    from concourse.bass_utils import run_bass_kernel_spmd

    a = {k: np.asarray(v) for k, v in inputs.items()}

    def edges(v, fill):
        rest = np.full((PADDED - EDGES,) + v.shape[1:], fill, v.dtype)
        return np.concatenate([v, rest])

    def by_tile(v, fill):
        return np.ascontiguousarray(edges(v, fill).reshape(TILES, P).T)

    x = np.concatenate([a["x"], np.zeros((NPAD - NODES, HID), np.float32)])
    laid = {
        "xT": np.ascontiguousarray(x.T),
        "xb": np.ascontiguousarray(x.reshape(BLOCKS, NB, HID).transpose(1, 0, 2)),
        "src": by_tile(a["src"], NODES),
        "dst": by_tile(a["dst"], 0),
        "dst_steps": edges(a["dst"], NODES - 1).reshape(STEPS, SE),
        "weight": by_tile(a["edge_weight"], 0),
        "fT": np.ascontiguousarray(edges(a["edge_attr_32"], 0).reshape(
            STEPS, 2, SE // 2, RBF).transpose(0, 1, 3, 2).reshape(STEPS, 2 * RBF, SE // 2)),
        "bond": np.ascontiguousarray(edges(a["edge_attr_16"], 0).reshape(STEPS, STEP, P, BOND).transpose(
            0, 2, 1, 3).reshape(STEPS, P, STEP * BOND)),
    }
    for name in ("w_in", "b_in", "w_f1", "b_f1", "w_f2", "b_f2", "w_o1", "b_o1", "w_o2", "b_o2"):
        laid[name] = np.ascontiguousarray(a["L0_gnn_" + name])
    for name in ("W1", "b1", "W2", "b2"):
        laid[name] = np.ascontiguousarray(a["L1_gnn_" + name])
    nc = bacc.Bacc("TRN2", target_bir_lowering=False, num_devices=1)
    args = {k: nc.dram_tensor("in_" + k, v.shape, mybir.dt.from_np(v.dtype), kind="ExternalInput").ap()
            for k, v in laid.items()}
    out = nc.dram_tensor("out", _OUT[0], F32, kind="ExternalOutput").ap()
    build(nc, out=out, **args)
    r = run_bass_kernel_spmd(nc, [{"in_" + k: v for k, v in laid.items()}], core_ids=[0])
    return r.results[0]["out"]
```
